# Optimizing a Trainium2 kernel written in Bass

```python
import numpy as np
import jax
import jax.numpy as jnp

def _softmax(x, axis=-1):
    return jax.nn.softmax(x, axis=axis)

def _gelu(x):
    return jax.nn.gelu(x, approximate=True)

def _silu(x):
    return jax.nn.silu(x)

def _sigmoid(x):
    return jax.nn.sigmoid(x)

def _layernorm(x, axis=-1, eps=1e-05):
    m = jnp.mean(x, axis=axis, keepdims=True)
    v = jnp.var(x, axis=axis, keepdims=True)
    return (x - m) / jnp.sqrt(v + eps)

def _scatter_add(tgt, idx, src, axis=0):
    return tgt.at[idx].add(src)

def _segment_sum(src, seg, n):
    return jax.ops.segment_sum(src, seg, n)
kernel_name = 'mk_seq_postln_d1_jaxref_r4_7d7797'

def setup_inputs(seed: int=0):
    np.random.seed(seed)
    _w = jnp.asarray

    def _L0_attn_setup():
        import jax, jax.numpy as jnp
        import numpy as np
        EMBED_DIM = 256
        NUM_HEADS = 16
        BLOCK_SIZE = 128
        GLOBAL_EVERY = 24

        def make_block_sparse_mask(seq_len):
            bi = jnp.arange(seq_len) // BLOCK_SIZE
            is_global = bi % GLOBAL_EVERY == 0
            allowed = (bi[:, None] == bi[None, :]) | is_global[:, None] | is_global[None, :]
            return jnp.where(allowed, 0.0, -jnp.inf).astype(jnp.float32)
        key = jax.random.key(seed)
        k_x, k_w, k_wo = jax.random.split(key, 3)
        B, L, D = (1, 1024, EMBED_DIM)
        x = jax.random.normal(k_x, (B, L, D), dtype=jnp.float32)
        w_qkv = jax.random.normal(k_w, (3 * D, D), dtype=jnp.float32) * 0.02
        b_qkv = jnp.zeros((3 * D,), dtype=jnp.float32)
        w_out = jax.random.normal(k_wo, (D, D), dtype=jnp.float32) * 0.02
        b_out = jnp.zeros((D,), dtype=jnp.float32)
        return {'x': x, 'w_qkv': w_qkv, 'b_qkv': b_qkv, 'w_out': w_out, 'b_out': b_out}
    _L0_attn_in = _L0_attn_setup()

    def _L0_ffn_setup():
        import jax, jax.numpy as jnp
        import numpy as np
        B, S, D = (4, 128, 256)
        E, K, H = (64, 8, 64)
        ES, HS = (2, 512)
        key = jax.random.key(seed)
        ks = jax.random.split(key, 8)
        scale = 0.02
        rn = lambda k, shape, s: jax.random.normal(k, shape, jnp.float32) * s
        return {'x': rn(ks[0], (B, S, D), 1.0), 'router_w': rn(ks[1], (D, E), scale), 'router_b': jnp.zeros((E,), jnp.float32), 'w1': rn(ks[2], (E, D, H), scale), 'b1': jnp.zeros((E, H), jnp.float32), 'w2': rn(ks[3], (E, H, D), scale), 'b2': jnp.zeros((E, D), jnp.float32), 'sw1': rn(ks[4], (ES, D, HS), scale), 'sb1': jnp.zeros((ES, HS), jnp.float32), 'sw2': rn(ks[5], (ES, HS, D), scale), 'sb2': jnp.zeros((ES, D), jnp.float32)}
    _L0_ffn_in = _L0_ffn_setup()
    _d = {'L0_attn_x': _L0_attn_in['x'], 'L0_attn_w_qkv': _L0_attn_in['w_qkv'], 'L0_attn_b_qkv': _L0_attn_in['b_qkv'], 'L0_attn_w_out': _L0_attn_in['w_out'], 'L0_attn_b_out': _L0_attn_in['b_out'], 'L0_ffn_router_w': _L0_ffn_in['router_w'], 'L0_ffn_router_b': _L0_ffn_in['router_b'], 'L0_ffn_w1': _L0_ffn_in['w1'], 'L0_ffn_b1': _L0_ffn_in['b1'], 'L0_ffn_w2': _L0_ffn_in['w2'], 'L0_ffn_b2': _L0_ffn_in['b2'], 'L0_ffn_sw1': _L0_ffn_in['sw1'], 'L0_ffn_sb1': _L0_ffn_in['sb1'], 'L0_ffn_sw2': _L0_ffn_in['sw2'], 'L0_ffn_sb2': _L0_ffn_in['sb2']}
    _x0 = _d['L0_attn_x']
    _d['L0_attn_x'] = jax.random.normal(jax.random.fold_in(jax.random.key(seed), 1), (4, 1024, 256), dtype=_x0.dtype)
    del _x0
    return _d

def reference(L0_attn_x, L0_attn_w_qkv, L0_attn_b_qkv, L0_attn_w_out, L0_attn_b_out, L0_ffn_router_w, L0_ffn_router_b, L0_ffn_w1, L0_ffn_b1, L0_ffn_w2, L0_ffn_b2, L0_ffn_sw1, L0_ffn_sb1, L0_ffn_sw2, L0_ffn_sb2):

    def _L0_attn_ref(x, w_qkv, b_qkv, w_out, b_out):
        import jax, jax.numpy as jnp
        import numpy as np
        EMBED_DIM = 256
        NUM_HEADS = 16
        BLOCK_SIZE = 128
        GLOBAL_EVERY = 24

        def make_block_sparse_mask(seq_len):
            bi = jnp.arange(seq_len) // BLOCK_SIZE
            is_global = bi % GLOBAL_EVERY == 0
            allowed = (bi[:, None] == bi[None, :]) | is_global[:, None] | is_global[None, :]
            return jnp.where(allowed, 0.0, -jnp.inf).astype(jnp.float32)
        B, L, D = x.shape
        H = NUM_HEADS
        hd = D // H
        mask = make_block_sparse_mask(L)
        qkv = x @ w_qkv.T + b_qkv
        q, k, v = jnp.split(qkv, 3, axis=-1)
        q = q.reshape(B, L, H, hd).transpose(0, 2, 1, 3)
        k = k.reshape(B, L, H, hd).transpose(0, 2, 1, 3)
        v = v.reshape(B, L, H, hd).transpose(0, 2, 1, 3)
        scale = 1.0 / jnp.sqrt(jnp.asarray(hd, dtype=x.dtype))
        scores = jnp.einsum('bhqd,bhkd->bhqk', q * scale, k) + mask
        attn = jax.nn.softmax(scores, axis=-1)
        out = jnp.einsum('bhqk,bhkd->bhqd', attn, v)
        out = out.transpose(0, 2, 1, 3).reshape(B, L, D)
        return out @ w_out.T + b_out

    def _L0_ffn_ref(x, router_w, router_b, w1, b1, w2, b2, sw1, sb1, sw2, sb2):
        import jax, jax.numpy as jnp
        import numpy as np
        B, S, D = (4, 128, 256)
        E, K, H = (64, 8, 64)
        ES, HS = (2, 512)
        b_, s_, d_ = x.shape
        xf = x.reshape(-1, d_)
        probs = jax.nn.softmax(xf @ router_w + router_b, axis=-1)
        tw, ti = jax.lax.top_k(probs, K)
        tw = tw / jnp.sum(tw, axis=-1, keepdims=True)

        def body(acc, p):
            W1, B1, W2, B2, e = p
            h = jax.nn.silu(xf @ W1 + B1) @ W2 + B2
            cw = jnp.sum(jnp.where(ti == e, tw, 0.0), axis=-1)
            return (acc + cw[:, None] * h, None)
        routed, _ = jax.lax.scan(body, jnp.zeros_like(xf), (w1, b1, w2, b2, jnp.arange(w1.shape[0])))

        def shared_mlp(W1, B1, W2, B2):
            return jax.nn.silu(xf @ W1 + B1) @ W2 + B2
        shared = jnp.sum(jax.vmap(shared_mlp)(sw1, sb1, sw2, sb2), axis=0)
        return (routed + shared).reshape(b_, s_, d_)
    x = L0_attn_x
    x = _layernorm(x + _L0_attn_ref(x, L0_attn_w_qkv, L0_attn_b_qkv, L0_attn_w_out, L0_attn_b_out), axis=-1)
    x = _layernorm(x + _L0_ffn_ref(x, L0_ffn_router_w, L0_ffn_router_b, L0_ffn_w1, L0_ffn_b1, L0_ffn_w2, L0_ffn_b2, L0_ffn_sw1, L0_ffn_sb1, L0_ffn_sw2, L0_ffn_sb2), axis=-1)
    return x

_drawn_inputs = setup_inputs


def setup_inputs(seed=0):
    import zlib

    import numpy as np

    out = dict(_drawn_inputs(seed))
    spreads = {'L0_attn_b_qkv': (0.0, 0.1),
     'L0_attn_b_out': (0.0, 0.1),
     'L0_ffn_router_b': (0.0, 0.401),
     'L0_ffn_b1': (0.0, 0.8),
     'L0_ffn_b2': (0.0, 0.1),
     'L0_ffn_sb1': (0.0, 0.1),
     'L0_ffn_sb2': (0.0, 0.1)}
    factors = {'L0_attn_w_qkv': 8.0, 'L0_ffn_w1': 6.144, 'L0_ffn_w2': 5.796}
    for name, (base, spread) in spreads.items():
        noise = np.random.default_rng([zlib.crc32(name.encode()), seed]).standard_normal(out[name].shape)
        drawn = base * np.exp(spread * noise) if base else spread * noise
        out[name] = jnp.asarray(drawn.astype(out[name].dtype))
    for name, factor in factors.items():
        out[name] = (out[name] * factor).astype(out[name].dtype)
    return out
```

```python
import concourse.bass as bass
from concourse import mybir
from contextlib import ExitStack


def post_ln_block_kernel(
    nc: bass.Bass,
    x: bass.AP,
    w_qkv: bass.AP,
    b_qkv: bass.AP,
    w_out: bass.AP,
    b_out: bass.AP,
    router_w: bass.AP,
    router_b: bass.AP,
    w1: bass.AP,
    b1: bass.AP,
    w2: bass.AP,
    b2: bass.AP,
    sw1: bass.AP,
    sb1: bass.AP,
    sw2: bass.AP,
    sb2: bass.AP,
    out: bass.AP,
):
    f32, f16, u32 = mybir.dt.float32, mybir.dt.float16, mybir.dt.uint32
    ALU = mybir.AluOpType
    ACT = mybir.ActivationFunctionType
    AX = mybir.AxisListType

    B, L, D = x.shape
    NH, HD = 16, 16
    TB = 128
    NB = L // TB
    KD = D // 128
    E, _, HE = w1.shape
    ES, _, HS = sw1.shape
    NR = E * HE // 128
    NC = NR + ES * HS // 128
    HID = NC * 128
    TOPK = 8
    NQ = 4
    GT = 512
    NG = L // GT
    GB = GT // TB
    EPS = 1e-5

    SX, SW, SQ, SC = 2.0**6, 2.0**8, 2.0**5, 2.0**4
    SROW = 2.0**10

    UNITS = [None, None] + [list(range(i, min(i + 2, NB))) for i in range(1, NB, 2)]
    NU = len(UNITS)
    SLOT = [0, 1, 0, 1]
    NSLOT = 2
    BEFORE = [SLOT[:q].count(SLOT[q]) for q in range(NQ)]
    PERB = [SLOT.count(s) for s in range(NSLOT)]
    STACK_DMAS, ROW_DMAS = 14, 4
    MU = 4 * NU
    STEPS = 2 * NU
    LEAD = 2
    RING = NQ * (MU + 1 + 2)
    SMALL = 30 * 16
    SETUP_DVE = 7 + 4 * NSLOT

    xt = x.rearrange("b (t p) d -> b p t d", p=TB)
    ot = out.rearrange("b (t p) d -> b p t d", p=TB)

    ctx = ExitStack()
    with ctx:
        def sb(name, shape, dt=f32):
            return ctx.enter_context(nc.sbuf_tensor(name, shape, dt))

        def sem(name):
            return ctx.enter_context(nc.semaphore(name))

        x_in = sb("x_in", [128, NB, D])
        y = sb("y", [128, NB, D])
        raw = [y[:, 4 * r:4 * r + 4, :].rearrange("p a d -> p (a d)") for r in range(2)]
        tok = sb("tok", [128, NB * D])
        tokh = tok[:, 0:1024].bitcast(f16).rearrange("p (k n) -> p k n", k=KD)
        tokl = tok[:, 1024:2048].bitcast(f16).rearrange("p (k n) -> p k n", k=KD)
        att = tok[:, :].rearrange("p (t d) -> p t d", t=NB)

        kq = sb("kq", [128, 5120])
        kh = kq[:, 0:1024].bitcast(f16).rearrange("p (c n) -> p c n", c=2)
        kl = kq[:, 1024:2048].bitcast(f16).rearrange("p (c n) -> p c n", c=2)
        qh = kq[:, 2048:3072].bitcast(f16).rearrange("p (c n) -> p c n", c=2)
        ql = kq[:, 3072:4096].bitcast(f16).rearrange("p (c n) -> p c n", c=2)
        proj = [kq[:, 4096 + 512 * r:4608 + 512 * r] for r in range(2)]
        ath = kq[:, 0:1024].bitcast(f16).rearrange("p (k n) -> p k n", k=KD)
        atl = kq[:, 1024:2048].bitcast(f16).rearrange("p (k n) -> p k n", k=KD)
        lg = kq[:, 2048:2560].rearrange("p (t e) -> p t e", t=NB)
        rest = kq[:, 2560:3072].rearrange("p (t e) -> p t e", t=NB)
        gate = kq[:, 3072:4096].rearrange("p (t e) -> p t e", t=NB)

        qs = [sb(f"qs{s}", [128, 2, L], f16) for s in range(NSLOT)]
        ks = [sb(f"ks{s}", [128, 4, L], f16) for s in range(NSLOT)]
        vs = sb("vs", [128, NB, NH, HD + 1])
        work = sb("work", [128, 5120])
        pt = [work[:, 2048 * r:2048 * r + 2048].rearrange("p (g n) -> p g n", g=4) for r in range(2)]
        hs_ = [work[:, 512 * r:512 * r + 512] for r in range(2)]
        hc = [work[:, 1024 + 512 * r:1536 + 512 * r] for r in range(4)]
        hh = [work[:, 3072 + 256 * r:3328 + 256 * r].bitcast(f16) for r in range(4)]
        hl = [work[:, 4096 + 256 * r:4352 + 256 * r].bitcast(f16) for r in range(4)]
        wraw = work[:, 0:2048].rearrange("p (j d) -> p j d", j=8)
        rraw = work[:, 2048:2176].rearrange("p (k e) -> p k e", k=KD)
        b2raw = work[:, 2304:2560]
        browraw = work[0:44, 2560:2688]
        sbraw = work[:, 2688:2944]
        oacc = sb("oacc", [128, L])

        w1h, w1l = sb("w1h", [128, KD, HID], f16), sb("w1l", [128, KD, HID], f16)
        w2h, w2l = sb("w2h", [128, NC, D], f16), sb("w2l", [128, NC, D], f16)
        wth, wtl = sb("wth", [128, KD, 1024], f16), sb("wtl", [128, KD, 1024], f16)
        rwh, rwl = sb("rwh", [128, KD, E], f16), sb("rwl", [128, KD, E], f16)
        b2h, b2l = sb("b2h", [128, D], f16), sb("b2l", [128, D], f16)
        bcol = sb("bcol", [128, NC + 4])
        bv, bo, sb2s = sb("bv", [128, D]), sb("bo", [128, D]), sb("sb2s", [128, D])
        rb = sb("rb", [128, E])
        sel = sb("sel", [128, NR, 128], f16)
        cwt = sb("cwt", [128, L], f16)
        ident = sb("ident", [128, 128])
        zero = sb("zero", [128, 128], f16)
        mxp = sb("mxp", [128, 4, 2])
        mx = sb("mx", [128, 4, NB])
        mrh, mrl = sb("mrh", [32, TB], f16), sb("mrl", [32, TB], f16)
        rc = sb("rc", [128, 2, 4, 4])
        bst = sb("bst", [128, NB, 6])
        mv = sb("mv", [128, NB, 2])
        std = sb("std", [128, NB])
        rstd = sb("rstd", [128, NB])
        rmax = sb("rmax", [128, NB])
        top = sb("top", [128, NB, TOPK])
        nsum = sb("nsum", [128, NB])

        ps = ctx.enter_context(nc.psum_tensor("ps", [128, 8, 512], f32))
        OUT0 = 6

        s_small = sem("small_weights_loaded")
        s_ident = sem("identity_ready")
        s_setup = sem("pool_setup_steps")
        s_raw = [sem(f"raw_weights_loaded{r}") for r in range(2)]
        s_wstep = sem("weight_split_steps")
        s_wt = sem("weights_transposed")
        s_wth = sem("transposed_weights_high")
        s_wtl = sem("transposed_weights_low")
        s_bias = sem("bias_columns_ready")
        s_init = sem("vector_setup_steps")
        s_wts = sem("expert_weights_ready")
        s_x = sem("x_loaded")
        s_xt, s_xh, s_xl = sem("x_transposed"), sem("x_high"), sem("x_low")
        s_prj, s_q32 = sem("projected"), sem("projection_out_of_psum")
        s_qkh, s_qkl, s_v = sem("qk_high"), sem("qk_low"), sem("values_ready")
        s_stk = [sem(f"stacks_loaded{s}") for s in range(NSLOT)]
        s_row = [sem(f"max_rows_loaded{s}") for s in range(NSLOT)]
        s_ring, s_free = sem("ring_filled"), sem("ring_read")
        s_mx = sem("maxima_ready")
        s_mrh = sem("max_rows_high")
        s_st, s_exp = sem("scores_ready"), sem("probabilities_ready")
        s_pv, s_oacc = sem("values_summed"), sem("quad_output_copied")
        s_rc = sem("reciprocal_sums_ready")
        s_at, s_ah, s_al = sem("attention_transposed"), sem("attention_high"), sem("attention_low")
        s_op = sem("output_projected")
        s_xb = sem("residual_ready")
        s_z, s_bs, s_ba = sem("ln1_sum_ready"), sem("ln1_stats"), sem("ln1_mean_var")
        s_var, s_std, s_rstd = sem("ln1_var"), sem("ln1_std"), sem("ln1_rstd")
        s_y = sem("ln1_done")
        s_yt, s_yh, s_yl = sem("y_transposed"), sem("y_high"), sem("y_low")
        s_yb = sem("ffn_residual_ready")
        s_lg, s_rt, s_e = sem("logits_ready"), sem("router_steps"), sem("router_exp_done")
        s_gt, s_cwh, s_cwl = sem("gates_transposed"), sem("gates_high"), sem("gates_low")
        s_u, s_cwb = sem("hidden_ready"), sem("gates_spread")
        s_silu, s_hc = sem("silu_done"), sem("hidden_gated")
        s_hh, s_hl = sem("hidden_high"), sem("hidden_low")
        s_dn = sem("down_done")
        s_ofree = sem("output_banks_free")
        s_z2, s_bs2, s_ba2 = sem("ln2_sum_ready"), sem("ln2_stats"), sem("ln2_mean_var")
        s_var2, s_std2, s_rstd2 = sem("ln2_var"), sem("ln2_std"), sem("ln2_rstd")
        s_n2 = sem("ln2_done")
        s_out = sem("output_stored")
        s_top, s_gate = sem("top8_steps"), sem("gates_ready")
        NR_ROUTER = 6

        block = ctx.enter_context(nc.Block())

        def blocks(ap, i):
            return ap.rearrange("p (a c) -> p a c", c=TB)[:, 0:i + 1:i, :]

        def place(pos):
            return pos // 2, pos % 2

        def ring_after_rows(q):
            return (q + 1) * (MU + 1) + 2 * max(0, q - 1)

        @block.sync
        def _(sp):
            wq = w_qkv[0:2 * D, :].rearrange("(j t c f) d -> j c t f d", j=2, t=4, c=2)
            for j in range(2):
                for c in range(2):
                    for t in range(4):
                        sp.dma_start(wraw[32 * t:32 * t + 32, 2 * j + c, :], wq[j, c, t, :, :])\
                          .then_inc(s_small, 16)
            sp.dma_start(wraw[:, 4:6, :], w_qkv[2 * D:3 * D, :].rearrange("(c p) d -> p c d", p=128))\
              .then_inc(s_small, 16)
            sp.dma_start(wraw[:, 6:8, :], w_out.rearrange("(c p) d -> p c d", p=128)).then_inc(s_small, 16)
            sp.dma_start(browraw[0:NR, :], b1.rearrange("(c a) h -> c (a h)", a=128 // HE)).then_inc(s_small, 16)
            sp.dma_start(browraw[NR:NC, :], sb1.rearrange("e (c h) -> (e c) h", h=128)).then_inc(s_small, 16)
            bq = b_qkv[0:2 * D].rearrange("(j t c f) -> j c t f", j=2, t=4, c=2)
            for j in range(2):
                sp.dma_start(browraw[NC + 2 * j:NC + 2 * j + 2, :].rearrange("c (t f) -> c t f", t=4), bq[j])\
                  .then_inc(s_small, 16)
            sp.dma_start(bv[:, :], b_qkv[2 * D:3 * D].partition_broadcast(128)).then_inc(s_small, 16)
            sp.dma_start(bo[:, :], b_out.partition_broadcast(128)).then_inc(s_small, 16)
            sp.dma_start(sb2s[:, :], sb2[0, :].partition_broadcast(128)).then_inc(s_small, 16)
            sp.dma_start(sbraw, sb2[1, :].partition_broadcast(128)).then_inc(s_small, 16)
            sp.dma_start(rb[:, :], router_b.partition_broadcast(128)).then_inc(s_small, 16)
            sp.dma_start(rraw, router_w.rearrange("(k p) e -> p k e", p=128)).then_inc(s_small, 16)
            for r in range(2):
                sp.dma_start(b2raw[E * r:E * r + E, :], b2).then_inc(s_small, 16)

            sp.wait_ge(s_init, SETUP_DVE)
            def apart(signal, value):
                value = sp.to_reg(value)
                sp.wait_ge(s_init, SETUP_DVE)
                sp.wait_ge(signal, value)

            with sp.Fori(0, B) as b:
                def stacks(q):
                    slot = SLOT[q]
                    for e in range(2):
                        s = 2 * q + e
                        for r, (k_part, q_part) in enumerate(((kh, qh), (kl, qh), (kh, ql))):
                            rows = slice(64 * e + 16 * r, 64 * e + 16 * r + 16)
                            sp.dma_start(ks[slot][rows, 2 * e:2 * e + 2, :], k_part[16 * s:16 * s + 16, :, :])\
                              .then_inc(s_stk[slot], 16)
                            sp.dma_start(qs[slot][rows, :, :], q_part[16 * s:16 * s + 16, :, :])\
                              .then_inc(s_stk[slot], 16)
                        sp.dma_start(qs[slot][64 * e + 48:64 * e + 50, :, :]
                                     .rearrange("p a (t c) -> p (a t) c", c=TB),
                                     zero[0:2, :].unsqueeze(1).to_broadcast([2, 2 * NB, TB]))\
                          .then_inc(s_stk[slot], 16)

                sp.wait_ge(s_qkl, b * 8 + 8)
                stacks(0)
                stacks(1)
                for q in range(NQ):
                    apart(s_mrh, b * NQ + q + 1)
                    apart(s_free, b * RING + ring_after_rows(q))
                    slot = SLOT[q]
                    for e in range(2):
                        for j, part in enumerate((mrh, mrl)):
                            sp.dma_start(qs[slot][64 * e + 48 + j:64 * e + 49 + j, :, :],
                                         part[16 * e:16 * e + 16, :]).then_inc(s_row[slot], 16)
                    if q + 2 < NQ:
                        sp.wait_ge(s_st, b * NQ * STEPS + (q + 1) * STEPS)
                        stacks(q + 2)
                for g in range(NG):
                    sp.wait_ge(s_n2, (b * NG + g) * GB + GB)
                    sp.dma_start(ot[b, :, g * GB:g * GB + GB, :] if isinstance(b, int) else
                                 ot[bass.ds(b, 1), :, g * GB:g * GB + GB, :].rearrange("o p t d -> (o p) t d"),
                                 y[:, g * GB:g * GB + GB, :]).then_inc(s_out, 16)
                apart(s_out, b * NG * 16 + NG * 16)

        PIECES = [("w1", k, e0) for k in range(KD) for e0 in range(0, E, 16)]
        PIECES += [("sw1", k, 0) for k in range(KD)]
        PIECES += [("w2", c, 0) for c in range(0, NR, 4)] + [("sw2", c, 0) for c in range(0, NC - NR, 4)]
        w2r = w2.rearrange("(c a) h d -> (a h) c d", a=128 // HE)
        sw2r = sw2.rearrange("e (c p) d -> p (e c) d", p=128)

        def split_target(kind, i, j):
            if kind == "w1":
                cols = slice(j * HE, j * HE + 1024)
                return w1h[:, i, cols], w1l[:, i, cols]
            if kind == "sw1":
                return w1h[:, i, NR * 128:HID], w1l[:, i, NR * 128:HID]
            c = i if kind == "w2" else NR + i
            return (w[:, c:c + 4, :].rearrange("p c d -> p (c d)") for w in (w2h, w2l))

        @block.gpsimd
        def _(pool):
            def load_x(b):
                pool.dma_start(x_in[:, :, :], xt[b] if isinstance(b, int) else
                               xt[bass.ds(b, 1)].rearrange("o p t d -> (o p) t d")).then_inc(s_x, 16)

            def load_piece(n):
                kind, i, j = PIECES[n]
                dst = raw[n % 2]
                if kind == "w1":
                    pool.dma_start(dst.rearrange("p (e h) -> p e h", h=HE),
                                   w1[j:j + 16, 128 * i:128 * i + 128, :].rearrange("e p h -> p e h"))\
                        .then_inc(s_raw[n % 2], 16)
                elif kind == "sw1":
                    pool.dma_start(dst.rearrange("p (e h) -> p e h", h=HS),
                                   sw1[:, 128 * i:128 * i + 128, :].rearrange("e p h -> p e h"))\
                        .then_inc(s_raw[n % 2], 16)
                else:
                    src = w2r if kind == "w2" else sw2r
                    pool.dma_start(dst.rearrange("p (c d) -> p c d", d=D), src[:, i:i + 4, :])\
                        .then_inc(s_raw[n % 2], 16)

            load_x(0)
            load_piece(0)
            load_piece(1)
            pool.memset(ident[:, :], 0.0).then_inc(s_setup, 1)
            pool.memset(sel[:, :, :], 0.0).then_inc(s_setup, 1)
            pool.wait_ge(s_setup, 2)
            pool.affine_select(out=ident[:, :], in_=ident[:, :], compare_op=ALU.not_equal, fill=1.0,
                               base=0, pattern=[[-1, 128]], channel_multiplier=1).then_inc(s_ident, 1)
            sel_e = sel[:, :, :].rearrange("p c (a h) -> p (c a) h", h=HE)
            for n, base in enumerate((0, -E)):
                pool.affine_select(out=sel_e, in_=sel_e, compare_op=ALU.not_equal, fill=1.0, base=base,
                                   pattern=[[-1, E], [0, HE]], channel_multiplier=1).then_inc(s_setup, 1)
                pool.wait_ge(s_setup, 3 + n)
            for n in range(len(PIECES)):
                high, low = split_target(*PIECES[n])
                pool.wait_ge(s_raw[n % 2], 16 * (n // 2 + 1))
                pool.tensor_scalar(raw[n % 2], raw[n % 2], SW, 1.0, ALU.mult, ALU.mult).then_inc(s_wstep, 1)
                pool.wait_ge(s_wstep, 3 * n + 1)
                pool.tensor_copy(high, raw[n % 2]).then_inc(s_wstep, 1)
                pool.wait_ge(s_wstep, 3 * n + 2)
                pool.tensor_tensor(low, raw[n % 2], high, ALU.subtract).then_inc(s_wstep, 1)
                pool.wait_ge(s_wstep, 3 * n + 3)
                if n + 2 < len(PIECES):
                    load_piece(n + 2)

            def batch(b, more):
                pool.wait_ge(s_small, SMALL)
                pool.wait_ge(s_x, b * 16 + 16)
                pool.wait_ge(s_xt, b * 4 + 4)
                pool.tensor_tensor(x_in[:, :, :], x_in[:, :, :], bo[:, :].unsqueeze(1).to_broadcast([128, NB, D]),
                                   ALU.add).then_inc(s_xb, 1)
                pool.wait_ge(s_z, b * NB + NB)
                if more:
                    load_x(b + 1)
                pool.wait_ge(s_y, b * NB + NB)
                pool.wait_ge(s_yt, b * 4 + 4)
                pool.wait_ge(s_init, SETUP_DVE)
                pool.tensor_tensor(y[:, :, :], y[:, :, :], sb2s[:, :].unsqueeze(1).to_broadcast([128, NB, D]),
                                   ALU.add).then_inc(s_yb, 1)

            with pool.Fori(0, B - 1) as b:
                batch(b, True)
            batch(B - 1, False)

        @block.scalar
        def _(act):
            def high_parts(dst, src_ready, base, done, scale):
                for n in range(4):
                    k, half = n % 2, n // 2
                    act.wait_ge(src_ready, base + n + 1)
                    act.activation(dst[:, k, 512 * half:512 * half + 512], ps[:, n, :], ACT.Copy, scale=scale)\
                       .then_inc(done, 1)

            high_parts(wth, s_wt, 0, s_wth, SW)
            act.wait_ge(s_wt, 5)
            act.activation(bcol[:, 0:NC], ps[:, 4, 0:NC], ACT.Copy).then_inc(s_bias, 1)
            act.activation(bcol[:, NC:NC + 4], ps[:, 4, NC:NC + 4], ACT.Copy, scale=SQ).then_inc(s_bias, 1)
            act.wait_ge(s_bias, 2)

            with act.Fori(0, B) as b:
                high_parts(tokh, s_xt, b * 4, s_xh, SX)
                for n in range(8):
                    j = (2, 2, 3, 3, 0, 0, 1, 1)[n]
                    act.wait_ge(s_prj, b * 12 + n + 1)
                    if n >= 2:
                        act.wait_ge(s_qkl, b * 8 + n - 1)
                    act.activation(proj[n % 2], ps[:, 4 + n % 4, :], ACT.Identity,
                                   bias=bcol[:, NC + j:NC + j + 1], scale=SQ / (SX * SW)).then_inc(s_q32, 1)
                for it in range(NQ + 1):
                    if it >= 1:
                        for s in range(STEPS):
                            n = (it - 1) * STEPS + s
                            u, hp = s // 2, s % 2
                            unit = (it - 1) * NU + u
                            w = 512 if UNITS[u] is None else 256 * len(UNITS[u])
                            act.wait_ge(s_st, b * NQ * STEPS + n + 1)
                            if unit >= 2:
                                act.wait_ge(s_pv, b * NQ * NU + unit - 1)
                            act.activation(pt[unit % 2][:, 2 * hp:2 * hp + 2, 0:w],
                                           ps[:, 2 + 2 * (n % 2):4 + 2 * (n % 2), 0:w], ACT.Exp,
                                           scale=HD**-0.5 / SQ**2).then_inc(s_exp, 1)
                        act.wait_ge(s_pv, b * NQ * NU + it * NU)
                        act.activation(oacc[:, :].rearrange("p (a n) -> p a n", a=2), ps[:, OUT0:OUT0 + 2, :],
                                       ACT.Copy).then_inc(s_oacc, 1)
                    if it < NQ:
                        act.wait_ge(s_ring, b * RING + ring_after_rows(it))
                        if it >= 1:
                            p = it - 1
                            act.wait_ge(s_row[SLOT[p]], (b * PERB[SLOT[p]] + BEFORE[p] + 1) * 16 * ROW_DMAS)
                        act.activation(mrh[:, :], ps[0:32, (ring_after_rows(it) - 1) % 2, 0:TB], ACT.Copy,
                                       scale=-1.0 / SROW).then_inc(s_mrh, 1)
                high_parts(ath, s_at, b * 4, s_ah, SX)
                act.wait_ge(s_var, b + 1)
                act.activation(std[:, :], mv[:, :, 1], ACT.Sqrt).then_inc(s_std, 1)
                high_parts(tokh, s_yt, b * 4, s_yh, SX)
                act.wait_ge(s_rt, b * NR_ROUTER + 3)
                act.activation(lg[:, :, :], lg[:, :, :], ACT.Exp).then_inc(s_e, 1)
                for n in range(2):
                    act.wait_ge(s_gt, b * 2 + n + 1)
                    act.activation(cwt[:, 512 * n:512 * n + 512], ps[:, 4 + n, :], ACT.Copy, scale=SC)\
                       .then_inc(s_cwh, 1)

                with act.Fori(0, NG) as g:
                    fi = b * NG + g

                    def silu(c, j, routed, first=False):
                        act.wait_ge(s_u, fi * NC + c + 1)
                        if not first:
                            if routed:
                                act.wait_ge(s_hc, fi * NR + c - 1)
                            else:
                                act.wait_ge(s_hl, fi * NC + c - 1)
                        bias = bcol[:, c:c + 1] if isinstance(c, int) else bcol[:, bass.ds(c, 1)]
                        act.activation(hs_[j % 2], ps[:, j % 2, :], ACT.Silu, bias=bias,
                                       scale=1.0 / (SX * SW)).then_inc(s_silu, 1)

                    def high(c, j, routed, first=False):
                        if routed:
                            act.wait_ge(s_hc, fi * NR + c + 1)
                        if not first:
                            act.wait_ge(s_dn, fi * NC + c - 3)
                        if routed:
                            act.activation(hh[j % 4], hc[j % 4], ACT.Copy).then_inc(s_hh, 1)
                        else:
                            act.wait_ge(s_silu, fi * NC + c + 1)
                            act.activation(hh[j % 4], hs_[j % 2], ACT.Copy, scale=SC).then_inc(s_hh, 1)

                    silu(0, 0, True, True)
                    for c in range(4):
                        silu(c + 1, c + 1, True, c == 0)
                        high(c, c, True, True)
                    with act.Fori(1, NR // 4 - 1) as it:
                        for j in range(4):
                            silu(it * 4 + j + 1, j + 1, True)
                            high(it * 4 + j, j, True)
                    for c in range(NR - 4, NC):
                        if c + 1 < NC:
                            silu(c + 1, c + 1, c + 1 < NR + 2)
                        high(c, c, c < NR)
                    act.wait_ge(s_var2, fi + 1)
                    act.activation(std[:, 0:GB], mv[:, 0:GB, 1], ACT.Sqrt).then_inc(s_std2, 1)

        @block.vector
        def _(dve):
            steps = [0]

            def init(ins):
                steps[0] += 1
                ins.then_inc(s_init, 1)

            def apart(signal, value):
                value = dve.to_reg(value)
                dve.wait_ge(s_init, SETUP_DVE)
                dve.wait_ge(signal, value)

            def low_parts(dst, high, high_done, base, done, scale):
                for n in range(4):
                    k, half = n % 2, n // 2
                    cols = slice(512 * half, 512 * half + 512)
                    dve.wait_ge(high_done, base + n + 1)
                    dve.scalar_tensor_tensor(dst[:, k, cols], ps[:, n, :], scale, high[:, k, cols],
                                             ALU.mult, ALU.subtract).then_inc(done, 1)

            for s in range(NSLOT):
                init(dve.memset(ks[s][:, :, :].rearrange("p a n -> p (a n)").bitcast(u32), 0))
                init(dve.memset(qs[s][:, :, :].rearrange("p a n -> p (a n)").bitcast(u32), 0))
            init(dve.memset(zero[:, :], 0.0))
            init(dve.memset(vs[:, :, :, :].rearrange("p t h d -> p (t h) d")[:, :, HD:HD + 1], 1.0))
            dve.memset(ps[:, OUT0:OUT0 + 2, :], 0.0).then_inc(s_ofree, 1)
            dve.wait_ge(s_init, 2 * NSLOT)
            for s in range(NSLOT):
                for e in range(2):
                    init(dve.memset(ks[s][64 * e + 32:64 * e + 64, 2 * e:2 * e + 2, :], SROW))
            dve.wait_ge(s_small, SMALL)
            init(dve.tensor_tensor(sb2s[:, :], sb2s[:, :], sbraw, ALU.add))
            init(dve.tensor_scalar(rwh[:, :, :], rraw, SW, None, ALU.mult))
            init(dve.tensor_scalar(b2h[:, :], b2raw, SW, None, ALU.mult))
            dve.wait_ge(s_init, steps[0])
            init(dve.scalar_tensor_tensor(rwl[:, :, :], rraw, SW, rwh[:, :, :], ALU.mult, ALU.subtract))
            init(dve.scalar_tensor_tensor(b2l[:, :], b2raw, SW, b2h[:, :], ALU.mult, ALU.subtract))
            assert steps[0] == SETUP_DVE
            low_parts(wtl, wth, s_wth, 0, s_wtl, SW)

            with dve.Fori(0, B) as b:
                low_parts(tokl, tokh, s_xh, b * 4, s_xl, SX)
                for n in range(8):
                    c, half = (n // 2) % 2, n % 2
                    high, low = (kh, kl) if n < 4 else (qh, ql)
                    cols = slice(512 * half, 512 * half + 512)
                    dve.wait_ge(s_q32, b * 8 + n + 1)
                    dve.tensor_copy(high[:, c, cols], proj[n % 2]).then_inc(s_qkh, 1)
                    dve.wait_ge(s_qkh, b * 8 + n + 1)
                    dve.tensor_tensor(low[:, c, cols], proj[n % 2], high[:, c, cols], ALU.subtract)\
                       .then_inc(s_qkl, 1)
                for t in range(NB):
                    dve.wait_ge(s_prj, b * 12 + 8 + t // 2 + 1)
                    dve.scalar_tensor_tensor(
                        vs[:, t, :, 0:HD],
                        ps[:, 4 + t // 2, 256 * (t % 2):256 * (t % 2) + 256].rearrange("p (h d) -> p h d", d=HD),
                        1.0 / (SX * SW), bv[:, :].rearrange("p (h d) -> p h d", d=HD),
                        ALU.mult, ALU.add).then_inc(s_v, 1)

                ring = 0

                def normalize(q, half):
                    o = ps[:, ring % 2, :].rearrange("p (t g d) -> p t g d", t=4, g=4)
                    n = 2 * q + half
                    dve.wait_ge(s_ring, b * RING + ring + 1)
                    dve.reciprocal(rc[:, half, :, :], o[:, :, :, HD]).then_inc(s_rc, 1)
                    dve.wait_ge(s_rc, b * 2 * NQ + n + 1)
                    dve.tensor_tensor(
                        att[:, 4 * half:4 * half + 4, 64 * q:64 * q + 64].rearrange("p t (g d) -> p t g d", g=4),
                        o[:, :, :, 0:HD], rc[:, half, :, :].unsqueeze(3).to_broadcast([128, 4, 4, HD]),
                        ALU.mult).then_inc(s_free, 1)

                for it in range(NQ + 1):
                    for s in range(STEPS):
                        if it < NQ:
                            for m in (2 * s, 2 * s + 1):
                                pos, u = m // NU, m % NU
                                dve.wait_ge(s_ring, b * RING + ring + 1)
                                if UNITS[u] is None:
                                    dst, src = mxp[:, pos, u:u + 1], ps[:, ring % 2, :]
                                else:
                                    k = len(UNITS[u])
                                    dst = mx[:, pos, UNITS[u][0]:UNITS[u][0] + k]
                                    src = ps[:, ring % 2, 0:256 * k].rearrange("p (a n) -> p a n", n=256)
                                dve.reduce_max(dst, src, axis=AX.X).then_inc(s_free, 1)
                                ring += 1
                        if s == 1 and it >= 2:
                            for half in range(2):
                                normalize(it - 2, half)
                                ring += 1
                    if it < NQ:
                        dve.wait_ge(s_free, b * RING + ring)
                        dve.tensor_reduce(mx[:, :, 0:1].rearrange("p g o -> p (g o)"), mxp[:, :, :],
                                          axis=AX.X, op=ALU.max).then_inc(s_mx, 1)
                        dve.wait_ge(s_mrh, b * NQ + it + 1)
                        dve.scalar_tensor_tensor(mrl[:, :], ps[0:32, ring % 2, 0:TB], -1.0 / SROW, mrh[:, :],
                                                 ALU.mult, ALU.subtract).then_inc(s_free, 1)
                        ring += 1
                        assert ring == ring_after_rows(it)
                for half in range(2):
                    normalize(NQ - 1, half)
                    ring += 1
                assert ring == RING

                low_parts(atl, ath, s_ah, b * 4, s_al, SX)
                dve.wait_ge(s_xb, b + 1)
                for t in range(NB):
                    dve.wait_ge(s_op, b * 4 + t // 2 + 1)
                    dve.scalar_tensor_tensor(y[:, t, :], ps[:, 4 + t // 2, 256 * (t % 2):256 * (t % 2) + 256],
                                             1.0 / (SX * SW), x_in[:, t, :], ALU.mult, ALU.add)\
                       .then_inc(s_z, 1)
                for t in range(NB):
                    dve.wait_ge(s_z, b * NB + t + 1)
                    dve.bn_stats(bst[:, t, :], y[:, t, :]).then_inc(s_bs, 1)
                for t in range(NB):
                    apart(s_bs, b * NB + t + 1)
                    dve.bn_aggr(mv[:, t, :], bst[:, t, :]).then_inc(s_ba, 1)
                dve.wait_ge(s_ba, b * NB + NB)
                dve.tensor_scalar(mv[:, :, 1], mv[:, :, 1], EPS, None, ALU.add).then_inc(s_var, 1)
                dve.wait_ge(s_std, b + 1)
                dve.reciprocal(rstd[:, :], std[:, :]).then_inc(s_rstd, 1)
                dve.wait_ge(s_rstd, b + 1)
                for t in range(NB):
                    dve.tensor_scalar(y[:, t, :], y[:, t, :], mv[:, t, 0:1], rstd[:, t:t + 1],
                                      ALU.subtract, ALU.mult).then_inc(s_y, 1)
                low_parts(tokl, tokh, s_yh, b * 4, s_yl, SX)

                dve.wait_ge(s_lg, b + 1)
                dve.scalar_tensor_tensor(lg[:, :, :], ps[:, 4, :].rearrange("p (t e) -> p t e", e=E),
                                         1.0 / (SX * SW), rb[:, :].unsqueeze(1).to_broadcast([128, NB, E]),
                                         ALU.mult, ALU.add).then_inc(s_rt, 1)
                dve.wait_ge(s_rt, b * NR_ROUTER + 1)
                dve.reduce_max(rmax[:, :], lg[:, :, :], axis=AX.X).then_inc(s_rt, 1)
                dve.wait_ge(s_rt, b * NR_ROUTER + 2)
                dve.tensor_tensor(lg[:, :, :], lg[:, :, :], rmax[:, :].unsqueeze(2).to_broadcast([128, NB, E]),
                                  ALU.subtract).then_inc(s_rt, 1)
                apart(s_e, b + 1)
                for t in range(NB):
                    dve.max(top[:, t, :], lg[:, t, :]).then_inc(s_top, 1)
                apart(s_top, b * 2 * NB + NB)
                for t in range(NB):
                    dve.match_replace(rest[:, t, :], top[:, t, :], lg[:, t, :], -1.0).then_inc(s_top, 1)
                dve.tensor_reduce(nsum[:, :], top[:, :, :], axis=AX.X, op=ALU.add, negate=True)\
                   .then_inc(s_rt, 1)
                dve.wait_ge(s_top, b * 2 * NB + 2 * NB)
                dve.wait_ge(s_rt, b * NR_ROUTER + 4)
                dve.reciprocal(nsum[:, :], nsum[:, :]).then_inc(s_rt, 1)
                dve.scalar_tensor_tensor(rest[:, :, :], rest[:, :, :], 0.0, lg[:, :, :],
                                         ALU.max, ALU.subtract).then_inc(s_rt, 1)
                dve.wait_ge(s_rt, b * NR_ROUTER + 6)
                for n in range(2):
                    dve.tensor_tensor(gate[:, :, E * n:E * n + E], rest[:, :, :],
                                      nsum[:, :].unsqueeze(2).to_broadcast([128, NB, E]), ALU.mult)\
                       .then_inc(s_gate, 1)
                for n in range(2):
                    cols = slice(512 * n, 512 * n + 512)
                    dve.wait_ge(s_cwh, b * 2 + n + 1)
                    dve.scalar_tensor_tensor(cwt[E:2 * E, cols], ps[E:2 * E, 4 + n, :], SC, cwt[E:2 * E, cols],
                                             ALU.mult, ALU.subtract).then_inc(s_cwl, 1)

                apart(s_yb, b + 1)
                with dve.Fori(0, NG) as g:
                    fi = b * NG + g

                    def gated(c, j):
                        dve.wait_ge(s_silu, fi * NC + c + 1)
                        dve.wait_ge(s_cwb, fi * NR + c + 1)
                        dve.tensor_tensor(hc[j % 4], hs_[j % 2], ps[:, 2 + j % 2, :], ALU.mult)\
                           .then_inc(s_hc, 1)

                    def low(c, routed, j):
                        dve.wait_ge(s_hh, fi * NC + c + 1)
                        if routed:
                            dve.tensor_tensor(hl[j % 4], hc[j % 4], hh[j % 4], ALU.subtract).then_inc(s_hl, 1)
                        else:
                            dve.scalar_tensor_tensor(hl[j % 4], hs_[j % 2], SC, hh[j % 4],
                                                     ALU.mult, ALU.subtract).then_inc(s_hl, 1)

                    gated(0, 0)
                    with dve.Fori(0, NR // 4 - 1) as it:
                        for j in range(4):
                            gated(it * 4 + j + 1, j + 1)
                            low(it * 4 + j, True, j)
                    for c in range(NR - 4, NC):
                        if c + 1 < NR:
                            gated(c + 1, c + 1)
                        low(c, c < NR, c)

                    dve.wait_ge(s_dn, fi * NC + NC)
                    for t in range(GB):
                        z = dve.scalar_tensor_tensor(
                            y[:, bass.ds(g * GB + t, 1), :].rearrange("p o d -> p (o d)"),
                            ps[:, OUT0 + t // 2, 256 * (t % 2):256 * (t % 2) + 256], 1.0 / (SC * SW),
                            y[:, bass.ds(g * GB + t, 1), :].rearrange("p o d -> p (o d)"), ALU.mult, ALU.add)
                        z.then_inc(s_z2 if t < GB - 1 else s_ofree, 1)
                    for t in range(GB):
                        if t < GB - 1:
                            apart(s_z2, fi * (GB - 1) + t + 1)
                        else:
                            apart(s_ofree, fi + 2)
                        dve.bn_stats(bst[:, t, :], y[:, bass.ds(g * GB + t, 1), :].rearrange("p o d -> p (o d)"))\
                           .then_inc(s_bs2, 1)
                    for t in range(GB):
                        apart(s_bs2, fi * GB + t + 1)
                        dve.bn_aggr(mv[:, t, :], bst[:, t, :]).then_inc(s_ba2, 1)
                    dve.wait_ge(s_ba2, fi * GB + GB)
                    dve.tensor_scalar(mv[:, 0:GB, 1], mv[:, 0:GB, 1], EPS, None, ALU.add).then_inc(s_var2, 1)
                    dve.wait_ge(s_std2, fi + 1)
                    dve.reciprocal(rstd[:, 0:GB], std[:, 0:GB]).then_inc(s_rstd2, 1)
                    dve.wait_ge(s_rstd2, fi + 1)
                    for t in range(GB):
                        yt_ = y[:, bass.ds(g * GB + t, 1), :].rearrange("p o d -> p (o d)")
                        dve.tensor_scalar(yt_, yt_, mv[:, t, 0:1], rstd[:, t:t + 1], ALU.subtract, ALU.mult)\
                           .then_inc(s_n2, 1)

        @block.tensor
        def _(pe):
            def transposed(src, done):
                for n in range(4):
                    k, half = n % 2, n // 2
                    for t in range(4):
                        last = pe.transpose(ps[:, n, 128 * t:128 * t + 128],
                                            src[:, 4 * half + t, 128 * k:128 * k + 128], ident[:, :])
                    last.then_inc(done, 1)

            def parts(dst, stationary, moving, start=True, stop=True, skip=False):
                terms = [(s, m) for k in range(len(stationary[0]))
                         for s, m in ((stationary[0][k], moving[0][k]), (stationary[0][k], moving[1][k]),
                                      (stationary[1][k], moving[0][k]))]
                for n, (s, m) in enumerate(terms):
                    last = pe.matmul(dst, s, m, start=start and n == 0, stop=stop and n == len(terms) - 1,
                                     skip_group_check=skip)
                return last

            pe.wait_ge(s_ident, 1)
            pe.wait_ge(s_small, SMALL)
            transposed(wraw, s_wt)
            pe.transpose(ps[:, 4, 0:NC + 4], browraw, ident[0:NC + 4, 0:NC + 4]).then_inc(s_wt, 1)
            pe.wait_ge(s_wtl, 4)
            pe.wait_ge(s_bias, 2)
            pe.wait_ge(s_init, SETUP_DVE)

            with pe.Fori(0, B) as b:
                pe.wait_ge(s_x, b * 16 + 16)
                transposed(x_in, s_xt)
                pe.wait_ge(s_xl, b * 4 + 4)
                for n in range(8):
                    j = (2, 2, 3, 3, 0, 0, 1, 1)[n]
                    half = n % 2
                    if n >= 4:
                        pe.wait_ge(s_q32, b * 8 + n - 3)
                    cols = slice(512 * half, 512 * half + 512)
                    parts(ps[:, 4 + n % 4, :],
                          [[w[:, k, 128 * j:128 * j + 128] for k in range(KD)] for w in (wth, wtl)],
                          [[m[:, k, cols] for k in range(KD)] for m in (tokh, tokl)]).then_inc(s_prj, 1)
                for t in range(NB):
                    if t % 2 == 0:
                        pe.wait_ge(s_q32, b * 8 + 4 + t // 2 + 1)
                    toks = slice(TB * t, TB * t + TB)
                    last = parts(ps[:, 4 + t // 2, 256 * (t % 2):256 * (t % 2) + 256],
                                 [[m[:, k, toks] for k in range(KD)] for m in (tokh, tokl)],
                                 [[w[:, k, 512:768] for k in range(KD)] for w in (wth, wtl)])
                    if t % 2:
                        last.then_inc(s_prj, 1)

                ring = 0

                def maxima_unit(q, m):
                    pos, u = m // NU, m % NU
                    pr = place(pos)[1]
                    slot = SLOT[q]
                    if ring >= 2:
                        pe.wait_ge(s_free, b * RING + ring - 1)
                    bank = ring % 2
                    if UNITS[u] is None:
                        last = pe.matmul(ps[:, bank, :], qs[slot][:, pr, 0:TB],
                                         ks[slot][:, pos, 512 * u:512 * u + 512], start=True, stop=True)
                    else:
                        for n, i in enumerate(UNITS[u]):
                            last = pe.matmul(ps[:, bank, 256 * n:256 * n + 256],
                                             qs[slot][:, pr, TB * i:TB * i + TB],
                                             blocks(ks[slot][:, pos, :], i), start=True, stop=True)
                    last.then_inc(s_ring, 1)

                def scores(q, s):
                    n = q * STEPS + s
                    u, hp = s // 2, s % 2
                    slot = SLOT[q]
                    if n >= 2:
                        pe.wait_ge(s_exp, b * NQ * STEPS + n - 1)
                    for a in range(2):
                        pos = 2 * hp + a
                        pr = place(pos)[1]
                        bank = 2 + 2 * (n % 2) + a
                        if UNITS[u] is None:
                            last = pe.matmul(ps[:, bank, :], ks[slot][:, pos, 0:TB],
                                             qs[slot][:, pr, 512 * u:512 * u + 512], start=True, stop=True)
                        else:
                            for m, i in enumerate(UNITS[u]):
                                last = pe.matmul(ps[:, bank, 256 * m:256 * m + 256],
                                                 ks[slot][:, pos, TB * i:TB * i + TB],
                                                 blocks(qs[slot][:, pr, :], i), start=True, stop=True)
                    last.then_inc(s_st, 1)

                def sum_values(q, u):
                    unit = q * NU + u
                    pe.wait_ge(s_exp, b * NQ * STEPS + q * STEPS + 2 * u + 2)
                    if u == 0 and q >= 1:
                        pe.wait_ge(s_oacc, b * NQ + q)
                    end = u == NU - 1
                    products = []
                    if UNITS[u] is None:
                        products.append((0, OUT0 + u, slice(0, 512), slice(0, 512), True, False))
                    else:
                        for m, i in enumerate(UNITS[u]):
                            bank, col = OUT0 + i // 4, TB * (i % 4)
                            products.append((i, OUT0, slice(0, TB), slice(256 * m, 256 * m + TB), False, end))
                            products.append((i, bank, slice(col, col + TB),
                                             slice(256 * m + TB, 256 * m + 256), False, end))
                    for i, bank, dst, src, start, stop in products:
                        for g in range(4):
                            pos = 2 * (g % 2) + g // 2
                            last = pe.matmul(ps[32 * g:32 * g + HD + 1, bank, dst], vs[:, i, 4 * q + g, :],
                                             pt[unit % 2][:, pos, src], start=start, stop=stop,
                                             skip_group_check=True)
                    last.then_inc(s_pv, 1)

                def output_back(q):
                    nonlocal ring
                    pe.wait_ge(s_oacc, b * NQ + q + 1)
                    for half in range(2):
                        pe.wait_ge(s_free, b * RING + ring - 1)
                        for t in range(4):
                            cols = slice(TB * (4 * half + t), TB * (4 * half + t) + TB)
                            last = pe.transpose(ps[:, ring % 2, TB * t:TB * t + TB], oacc[:, cols], ident[:, :])
                        last.then_inc(s_ring, 1)
                        ring += 1

                for it in range(NQ + 1):
                    for s in range(STEPS + LEAD):
                        if it < NQ and s < STEPS:
                            if s == 0:
                                pe.wait_ge(s_stk[SLOT[it]],
                                           (b * PERB[SLOT[it]] + BEFORE[it] + 1) * 16 * STACK_DMAS)
                            maxima_unit(it, 2 * s)
                            ring += 1
                            maxima_unit(it, 2 * s + 1)
                            ring += 1
                        if s == 1 and it >= 2:
                            output_back(it - 2)
                        if it >= 1 and s >= LEAD:
                            q, r = it - 1, s - LEAD
                            if r == 0:
                                if q == 0:
                                    pe.wait_ge(s_v, b * NB + NB)
                                pe.wait_ge(s_row[SLOT[q]],
                                           (b * PERB[SLOT[q]] + BEFORE[q] + 1) * 16 * ROW_DMAS)
                            scores(q, r)
                            if r % 2 and r >= 3:
                                sum_values(q, (r - 3) // 2)
                    if it >= 1:
                        sum_values(it - 1, NU - 1)
                    if it < NQ:
                        pe.wait_ge(s_mx, b * NQ + it + 1)
                        pe.wait_ge(s_free, b * RING + ring - 1)
                        pe.transpose(ps[0:32, ring % 2, 0:TB], mx[:, :, :].rearrange("p g t -> p (g t)"),
                                     ident[:, :]).then_inc(s_ring, 1)
                        ring += 1
                output_back(NQ - 1)
                assert ring == RING

                pe.wait_ge(s_free, b * RING + RING)
                transposed(att, s_at)
                pe.wait_ge(s_al, b * 4 + 4)
                for t in range(NB):
                    toks = slice(TB * t, TB * t + TB)
                    last = parts(ps[:, 4 + t // 2, 256 * (t % 2):256 * (t % 2) + 256],
                                 [[m[:, k, toks] for k in range(KD)] for m in (ath, atl)],
                                 [[w[:, k, 768:1024] for k in range(KD)] for w in (wth, wtl)])
                    if t % 2:
                        last.then_inc(s_op, 1)

                pe.wait_ge(s_y, b * NB + NB)
                transposed(y, s_yt)
                pe.wait_ge(s_yl, b * 4 + 4)
                for t in range(NB):
                    toks = slice(TB * t, TB * t + TB)
                    last = parts(ps[:, 4, E * t:E * t + E],
                                 [[m[:, k, toks] for k in range(KD)] for m in (tokh, tokl)],
                                 [[w[:, k, :] for k in range(KD)] for w in (rwh, rwl)])
                last.then_inc(s_lg, 1)
                pe.wait_ge(s_gate, b * 2 + 2)
                for n in range(2):
                    for t in range(4):
                        last = pe.transpose(ps[:, 4 + n, TB * t:TB * t + TB], gate[:, 4 * n + t, :], ident[:, :])
                    last.then_inc(s_gt, 1)
                pe.wait_ge(s_wstep, 3 * len(PIECES))
                pe.wait_ge(s_setup, 4)
                pe.wait_ge(s_cwl, b * 2 + 2)

                with pe.Fori(0, NG) as g:
                    fi = b * NG + g

                    def tokens(m, k):
                        return m[:, k, bass.ds(g * GT, GT)]

                    def up(c, j, routed, first=False):
                        if isinstance(c, int):
                            cols = slice(128 * c, 128 * c + 128)
                        else:
                            cols = bass.ds(c * 128, 128)
                        if not first:
                            pe.wait_ge(s_silu, fi * NC + c - 1)
                        parts(ps[:, j % 2, :], [[w[:, k, cols] for k in range(KD)] for w in (w1h, w1l)],
                              [[tokens(m, k) for k in range(KD)] for m in (tokh, tokl)]).then_inc(s_u, 1)
                        if routed:
                            if not first:
                                pe.wait_ge(s_hc, fi * NR + c - 1)
                            one = sel[:, c, :] if isinstance(c, int) else \
                                sel[:, bass.ds(c, 1), :].rearrange("p o m -> p (o m)")
                            pe.matmul(ps[:, 2 + j % 2, :], one, cwt[:, bass.ds(g * GT, GT)],
                                      start=True, stop=True).then_inc(s_cwb, 1)

                    def down(c, j, end=False):
                        pe.wait_ge(s_hl, fi * NC + c + 1)
                        for t in range(GB):
                            toks = slice(TB * t, TB * t + TB)
                            if isinstance(c, int):
                                ws = [w[:, c, :] for w in (w2h, w2l)]
                            else:
                                ws = [w[:, bass.ds(c, 1), :].rearrange("p o d -> p (o d)") for w in (w2h, w2l)]
                            last = parts(ps[:, OUT0 + t // 2, 256 * (t % 2):256 * (t % 2) + 256],
                                         [[h[j % 4][:, toks]] for h in (hh, hl)], [[w] for w in ws],
                                         start=False, stop=end, skip=True)
                        last.then_inc(s_dn, 1)

                    up(0, 0, True, True)
                    up(1, 1, True, True)
                    pe.wait_ge(s_ofree, fi + 1)
                    for t in range(GB):
                        toks = cwt[:, bass.ds(g * GT + TB * t, TB)]
                        dst = ps[:, OUT0 + t // 2, 256 * (t % 2):256 * (t % 2) + 256]
                        pe.matmul(dst, toks, b2h[:, :], start=t % 2 == 0, stop=False, skip_group_check=True)
                        pe.matmul(dst, toks, b2l[:, :], start=False, stop=False, skip_group_check=True)
                    with pe.Fori(0, NR // 4 - 1) as it:
                        for j in range(4):
                            up(it * 4 + j + 2, j, True)
                            down(it * 4 + j, j)
                    for c in range(NR - 4, NC):
                        if c + 2 < NC:
                            up(c + 2, c, c + 2 < NR)
                        down(c, c, c == NC - 1)


_INS = ['L0_attn_x', 'L0_attn_w_qkv', 'L0_attn_b_qkv', 'L0_attn_w_out', 'L0_attn_b_out',
        'L0_ffn_router_w', 'L0_ffn_router_b', 'L0_ffn_w1', 'L0_ffn_b1', 'L0_ffn_w2', 'L0_ffn_b2',
        'L0_ffn_sw1', 'L0_ffn_sb1', 'L0_ffn_sw2', 'L0_ffn_sb2']
_OUTS = [((4, 1024, 256), 'float32')]


def kernel(**inputs):
    import numpy as _np
    import concourse.bacc as _bacc
    from concourse import mybir as _mybir
    from concourse.bass_utils import run_bass_kernel_spmd as _run

    nc = _bacc.Bacc("TRN2", target_bir_lowering=False, num_devices=1)
    arrays, args = {}, []
    for name in _INS:
        a = _np.ascontiguousarray(inputs[name])
        arrays[f"in_{name}_dram"] = a
        args.append(nc.dram_tensor(f"in_{name}_dram", a.shape, _mybir.dt.from_np(a.dtype), kind="ExternalInput").ap())
    for i, (shape, dtype) in enumerate(_OUTS):
        dt = _mybir.dt.from_np(_np.dtype(dtype))
        args.append(nc.dram_tensor(f"out_{i}_dram", shape, dt, kind="ExternalOutput").ap())
    post_ln_block_kernel(nc, *args)
    r = _run(nc, [arrays], core_ids=[0])
    return r.results[0]["out_0_dram"]
```

```python
import concourse.bass as bass
from concourse import mybir
from contextlib import ExitStack


def post_ln_block_kernel(
    nc: bass.Bass,
    x: bass.AP,
    w_qkv: bass.AP,
    b_qkv: bass.AP,
    w_out: bass.AP,
    b_out: bass.AP,
    router_w: bass.AP,
    router_b: bass.AP,
    w1: bass.AP,
    b1: bass.AP,
    w2: bass.AP,
    b2: bass.AP,
    sw1: bass.AP,
    sb1: bass.AP,
    sw2: bass.AP,
    sb2: bass.AP,
    out: bass.AP,
):
    f32, f16, u32 = mybir.dt.float32, mybir.dt.float16, mybir.dt.uint32
    ALU = mybir.AluOpType
    ACT = mybir.ActivationFunctionType
    AX = mybir.AxisListType

    B, L, D = x.shape
    NH, HD = 16, 16
    TB = 128
    NB = L // TB
    KD = D // 128
    E, _, HE = w1.shape
    ES, _, HS = sw1.shape
    NR = E * HE // 128
    NS = ES * HS // 128
    NC = NS + NR
    HID = NC * 128
    TOPK = 8
    NQ = 4
    GT = 512
    NG = L // GT
    GB = GT // TB
    EPS = 1e-5

    SX, SW, SQ, SC = 2.0**6, 2.0**8, 2.0**5, 2.0**4
    SROW = 2.0**10

    UNITS = [None, None] + [list(range(i, min(i + 2, NB))) for i in range(1, NB, 2)]
    NU = len(UNITS)
    SLOT = [0, 1, 2, 0]
    NSLOT = 3
    BEFORE = [SLOT[:q].count(SLOT[q]) for q in range(NQ)]
    PERB = [SLOT.count(s) for s in range(NSLOT)]
    STACK_DMAS, ROW_DMAS = 10, 2
    MU = 4 * NU
    STEPS = 2 * NU
    GATES_AT = 4
    LEAD = 2
    ROWS_AT = STEPS + 1
    RING = NQ * (MU + 1 + 2) + 2
    FIRST, SMALL = 16 * 16, 6 * 16
    SETUP_DVE = 7 + 2 * NSLOT

    xt = x.rearrange("b (t p) d -> b p t d", p=TB)
    ot = out.rearrange("b (t p) d -> b p t d", p=TB)

    ctx = ExitStack()
    with ctx:
        def sb(name, shape, dt=f32):
            return ctx.enter_context(nc.sbuf_tensor(name, shape, dt))

        def sem(name):
            return ctx.enter_context(nc.semaphore(name))

        y = sb("y", [128, NB, D])
        raw = [y[:, 4 * r:4 * r + 4, :].rearrange("p a d -> p (a d)") for r in range(2)]
        tok = sb("tok", [128, NB * D])
        tokh = tok[:, 0:1024].bitcast(f16).rearrange("p (k n) -> p k n", k=KD)
        tokl = tok[:, 1024:2048].bitcast(f16).rearrange("p (k n) -> p k n", k=KD)
        att = tok[:, :].rearrange("p (t d) -> p t d", t=NB)

        kq = sb("kq", [128, 5120])
        kh = kq[:, 0:1024].bitcast(f16).rearrange("p (c n) -> p c n", c=2)
        kl = kq[:, 1024:2048].bitcast(f16).rearrange("p (c n) -> p c n", c=2)
        qh = kq[:, 2048:3072].bitcast(f16).rearrange("p (c n) -> p c n", c=2)
        ql = kq[:, 3072:4096].bitcast(f16).rearrange("p (c n) -> p c n", c=2)
        proj = [kq[:, 4096 + 512 * r:4608 + 512 * r] for r in range(2)]
        oacc = kq[:, 4096:5120]
        xs = kq[:, 3072:5120].rearrange("p (t d) -> p t d", t=NB)
        reph = kq[:, 2048:2176].bitcast(f16).rearrange("p (k m) -> p k m", k=KD)
        repl = kq[:, 2176:2304].bitcast(f16).rearrange("p (k m) -> p k m", k=KD)
        ath = kq[:, 0:1024].bitcast(f16).rearrange("p (k n) -> p k n", k=KD)
        atl = kq[:, 1024:2048].bitcast(f16).rearrange("p (k n) -> p k n", k=KD)
        lg = kq[:, 2048:2560].rearrange("p (t e) -> p t e", t=NB)
        untop = kq[:, 2560:3072].rearrange("p (t e) -> p t e", t=NB)
        gate = kq[:, 3072:4096].rearrange("p (t e) -> p t e", t=NB)

        qs = [sb(f"qs{s}", [128, 2, L], f16) for s in range(NSLOT)]
        ks = [sb(f"ks{s}", [128, 4, L], f16) for s in range(NSLOT)]
        vs = sb("vs", [128, NB, NH, HD + 1])
        work = sb("work", [128, 5120])
        pt = [work[:, 2048 * r:2048 * r + 2048].rearrange("p (g n) -> p g n", g=4) for r in range(2)]
        hs_ = [work[:, 512 * r:512 * r + 512] for r in range(2)]
        hc = [work[:, 1024 + 512 * r:1536 + 512 * r] for r in range(4)]
        hh = [work[:, 3072 + 256 * r:3328 + 256 * r].bitcast(f16) for r in range(4)]
        hl = [work[:, 4096 + 256 * r:4352 + 256 * r].bitcast(f16) for r in range(4)]
        wraw = work[:, 0:2048].rearrange("p (j d) -> p j d", j=8)
        rraw = work[:, 2048:2176].rearrange("p (k e) -> p k e", k=KD)
        b2raw = work[:, 2304:2560]
        browraw = work[0:NC + 6, 2560:2688]
        sbraw = work[:, 2688:2944]

        w1h, w1l = sb("w1h", [128, KD, HID], f16), sb("w1l", [128, KD, HID], f16)
        w2h, w2l = sb("w2h", [128, NC, D], f16), sb("w2l", [128, NC, D], f16)
        wth, wtl = sb("wth", [128, KD, 1024], f16), sb("wtl", [128, KD, 1024], f16)
        rwh, rwl = sb("rwh", [128, KD, E], f16), sb("rwl", [128, KD, E], f16)
        b2h, b2l = sb("b2h", [128, D], f16), sb("b2l", [128, D], f16)
        bcol = sb("bcol", [128, NC + 6])
        bo, sb2s = sb("bo", [128, D]), sb("sb2s", [128, D])
        rb = sb("rb", [128, E])
        sel = sb("sel", [128, NR, 128], f16)
        cwt = sb("cwt", [128, L], f16)
        ident = sb("ident", [128, 128])
        zero = sb("zero", [128, 128], f16)
        srow = sb("srow", [128, 128], f16)
        mxp = sb("mxp", [128, 4, 2])
        mx = sb("mx", [128, 4, NB])
        mrh, mrl = sb("mrh", [32, TB], f16), sb("mrl", [32, TB], f16)
        rc = sb("rc", [128, 2, 4, 4])
        bst = sb("bst", [128, NB, 6])
        mv = sb("mv", [128, NB, 2])
        std = sb("std", [128, NB])
        rstd = sb("rstd", [128, NB])
        nmr = sb("nmr", [128, NB])
        rmax = sb("rmax", [128, NB])
        top = sb("top", [128, NB, TOPK])
        nsum = sb("nsum", [128, NB])

        ps = ctx.enter_context(nc.psum_tensor("ps", [128, 8, 512], f32))
        OUT0 = 6

        s_first = sem("projection_weights_loaded")
        s_small = sem("small_weights_loaded")
        s_slot2 = sem("last_slot_zeroed")
        s_rows = sem("constant_rows_loaded")
        s_rep = sem("value_bias_high")
        s_bvo = sem("value_bias_projected")
        s_bo = sem("output_bias_ready")
        s_ident = sem("identity_ready")
        s_setup = sem("pool_setup_steps")
        s_raw = [sem(f"raw_weights_loaded{r}") for r in range(2)]
        s_wstep = sem("weight_split_steps")
        s_wt = sem("weights_transposed")
        s_wth = sem("transposed_weights_high")
        s_wtl = sem("transposed_weights_low")
        s_bias = sem("bias_columns_ready")
        s_init = sem("vector_setup_steps")
        s_wts = sem("expert_weights_ready")
        s_x = sem("x_loaded")
        s_xr = sem("x_residual_loaded")
        s_a0 = sem("first_features_high")
        s_xt, s_xh, s_xl = sem("x_transposed"), sem("x_high"), sem("x_low")
        s_prj, s_q32 = sem("projected"), sem("projection_out_of_psum")
        s_qkh, s_qkl, s_v = sem("qk_high"), sem("qk_low"), sem("values_ready")
        s_stk = [sem(f"stacks_loaded{s}") for s in range(NSLOT)]
        s_row = [sem(f"max_rows_loaded{s}") for s in range(NSLOT)]
        s_ring, s_free = sem("ring_filled"), sem("ring_read")
        s_mx = sem("maxima_ready")
        s_mrh = sem("max_rows_high")
        s_st, s_exp = sem("scores_ready"), sem("probabilities_ready")
        s_pv, s_oacc = sem("values_summed"), sem("quad_output_copied")
        s_rc = sem("reciprocal_sums_ready")
        s_at, s_ah, s_al = sem("attention_transposed"), sem("attention_high"), sem("attention_low")
        s_op = sem("output_projected")
        s_xb = sem("residual_ready")
        s_z, s_bs, s_ba = sem("ln1_sum_ready"), sem("ln1_stats"), sem("ln1_mean_var")
        s_var, s_std, s_rstd = sem("ln1_var"), sem("ln1_std"), sem("ln1_rstd")
        s_nm, s_nm2 = sem("ln1_shift"), sem("ln2_shift")
        s_y = sem("ln1_done")
        s_yt, s_yh, s_yl = sem("y_transposed"), sem("y_high"), sem("y_low")
        s_yb = sem("ffn_residual_ready")
        s_lg, s_rt, s_e = sem("logits_ready"), sem("router_steps"), sem("router_exp_done")
        s_gt, s_cwh, s_cwl = sem("gates_transposed"), sem("gates_high"), sem("gates_low")
        s_u, s_cwb = sem("hidden_ready"), sem("gates_spread")
        s_silu, s_hc = sem("silu_done"), sem("hidden_gated")
        s_hh, s_hl = sem("hidden_high"), sem("hidden_low")
        s_dn = sem("down_done")
        s_ofree = sem("output_banks_free")
        s_z2, s_bs2, s_ba2 = sem("ln2_sum_ready"), sem("ln2_stats"), sem("ln2_mean_var")
        s_var2, s_std2, s_rstd2 = sem("ln2_var"), sem("ln2_std"), sem("ln2_rstd")
        s_n2 = sem("ln2_done")
        s_out = sem("output_stored")
        s_top, s_gate = sem("top8_steps"), sem("gates_ready")
        NR_ROUTER = 6

        block = ctx.enter_context(nc.Block())

        def blocks(ap, i):
            return ap.rearrange("p (a c) -> p a c", c=TB)[:, 0:i + 1:i, :]

        def place(pos):
            return pos // 2, pos % 2

        def ring_after_rows(q):
            return (q + 1) * (MU + 1) + 2 * max(0, q - 1)

        def first_weights(eng, j):
            w = w_qkv[0:2 * D, :].rearrange("(j t c f) d -> j t f c d", j=2, t=4, c=2)
            for t in range(4):
                eng.dma_start(wraw[32 * t:32 * t + 32, 2 * j:2 * j + 2, :], w[j, t, :, :, :]).then_inc(s_first, 16)
            bias = b_qkv[0:2 * D].rearrange("(j t c f) -> j c t f", j=2, t=4, c=2)
            eng.dma_start(browraw[NC + 2 * j:NC + 2 * j + 2, :].rearrange("c (t f) -> c t f", t=4), bias[j])\
               .then_inc(s_first, 16)

        @block.sync
        def _(sp):
            first_weights(sp, 0)
            sp.dma_start(wraw[:, 4:6, :], w_qkv[2 * D:3 * D, :].rearrange("(c p) d -> p c d", p=128))\
              .then_inc(s_first, 16)
            sp.dma_start(browraw[NS:NC, :], b1.rearrange("(c a) h -> c (a h)", a=128 // HE)).then_inc(s_first, 16)
            sp.dma_start(browraw[0:NS, :], sb1.rearrange("e (c h) -> (e c) h", h=128)).then_inc(s_first, 16)
            sp.dma_start(sb2s[:, :], sb2[0, :].partition_broadcast(128)).then_inc(s_small, 16)
            sp.dma_start(sbraw, sb2[1, :].partition_broadcast(128)).then_inc(s_small, 16)
            sp.dma_start(rb[:, :], router_b.partition_broadcast(128)).then_inc(s_small, 16)
            sp.dma_start(rraw, router_w.rearrange("(k p) e -> p k e", p=128)).then_inc(s_small, 16)
            for r in range(2):
                sp.dma_start(b2raw[E * r:E * r + E, :], b2).then_inc(s_small, 16)

            sp.wait_ge(s_init, 2 * NSLOT + 1)
            sp.wait_ge(s_slot2, 1)
            for slot in range(NSLOT):
                for e in range(2):
                    for j in range(2):
                        row = 96 + e + 2 * j
                        sp.dma_start(ks[slot][row:row + 1, 2 * e:2 * e + 2, :]
                                     .rearrange("p a (t c) -> p (a t) c", c=TB),
                                     srow[0:1, :].unsqueeze(1).to_broadcast([1, 2 * NB, TB]))\
                          .then_inc(s_rows, 16)

            def apart(signal, value):
                value = sp.to_reg(value)
                sp.wait_ge(s_init, 2 * NSLOT + 1)
                sp.wait_ge(signal, value)

            def stack_k(q):
                slot = SLOT[q]
                for e in range(2):
                    src = slice(32 * q + 16 * e, 32 * q + 16 * e + 16)
                    for r, part in enumerate((kh, kl, kh)):
                        rows = slice(32 * r + 16 * e, 32 * r + 16 * e + 16)
                        sp.dma_start(ks[slot][rows, 2 * e:2 * e + 2, :], part[src, :, :])\
                          .then_inc(s_stk[slot], 16)
                sp.dma_start(qs[slot][96:100, :, :].rearrange("p a (t c) -> p (a t) c", c=TB),
                             zero[0:4, :].unsqueeze(1).to_broadcast([4, 2 * NB, TB]))\
                  .then_inc(s_stk[slot], 16)

            def stack_q(q):
                slot = SLOT[q]
                for r, part in enumerate((qh, qh, ql)):
                    sp.dma_start(qs[slot][32 * r:32 * r + 32, :, :], part[32 * q:32 * q + 32, :, :])\
                      .then_inc(s_stk[slot], 16)

            def front(b):
                sp.wait_ge(s_qkl, b * 8 + 4)
                stack_k(0)
                sp.wait_ge(s_qkl, b * 8 + 8)
                stack_q(0)
                for q in (1, 2):
                    stack_k(q)
                    stack_q(q)

            def rest(b):
                for q in range(NQ):
                    apart(s_mrh, b * NQ + q + 1)
                    apart(s_free, b * RING + ring_after_rows(q))
                    slot = SLOT[q]
                    for j, part in enumerate((mrh, mrl)):
                        sp.dma_start(qs[slot][96 + 2 * j:98 + 2 * j, :, :], part[:, :]).then_inc(s_row[slot], 16)
                    if q == 1:
                        sp.wait_ge(s_st, b * NQ * STEPS + STEPS)
                        stack_k(3)
                        stack_q(3)

            def store(b):
                for g in range(NG):
                    sp.wait_ge(s_n2, b * NB + (g + 1) * GB)
                    sp.dma_start(ot[b, :, g * GB:g * GB + GB, :] if isinstance(b, int) else
                                 ot[bass.ds(b, 1), :, g * GB:g * GB + GB, :].rearrange("o p t d -> (o p) t d"),
                                 y[:, g * GB:g * GB + GB, :]).then_inc(s_out, 16)

            front(0)
            with sp.Fori(0, B - 1) as b:
                rest(b)
                front(b + 1)
                store(b)
            rest(B - 1)
            store(B - 1)
            sp.wait_ge(s_rows, 4 * NSLOT * 16)
            sp.wait_ge(s_out, B * NG * 16)

        PIECES = [("w1", k, e0) for k in range(KD) for e0 in range(0, E, 16)]
        PIECES += [("sw1", k, 0) for k in range(KD)]
        PIECES += [("w2", c, 0) for c in range(0, NR, 4)] + [("sw2", c, 0) for c in range(0, NS, 4)]
        w2r = w2.rearrange("(c a) h d -> (a h) c d", a=128 // HE)
        sw2r = sw2.rearrange("e (c p) d -> p (e c) d", p=128)

        def split_target(kind, i, j):
            if kind == "w1":
                cols = slice(NS * 128 + j * HE, NS * 128 + j * HE + 1024)
                return w1h[:, i, cols], w1l[:, i, cols]
            if kind == "sw1":
                return w1h[:, i, 0:NS * 128], w1l[:, i, 0:NS * 128]
            c = NS + i if kind == "w2" else i
            return (w[:, c:c + 4, :].rearrange("p c d -> p (c d)") for w in (w2h, w2l))

        @block.gpsimd
        def _(pool):
            def load_x(dst, b, done):
                pool.dma_start(dst[:, :, :], xt[b] if isinstance(b, int) else
                               xt[bass.ds(b, 1)].rearrange("o p t d -> (o p) t d")).then_inc(done, 16)

            def load_piece(n):
                kind, i, j = PIECES[n]
                dst = raw[n % 2]
                if kind == "w1":
                    pool.dma_start(dst.rearrange("p (e h) -> p e h", h=HE),
                                   w1[j:j + 16, 128 * i:128 * i + 128, :].rearrange("e p h -> p e h"))\
                        .then_inc(s_raw[n % 2], 16)
                elif kind == "sw1":
                    pool.dma_start(dst.rearrange("p (e h) -> p e h", h=HS),
                                   sw1[:, 128 * i:128 * i + 128, :].rearrange("e p h -> p e h"))\
                        .then_inc(s_raw[n % 2], 16)
                else:
                    src = w2r if kind == "w2" else sw2r
                    pool.dma_start(dst.rearrange("p (c d) -> p c d", d=D), src[:, i:i + 4, :])\
                        .then_inc(s_raw[n % 2], 16)

            load_x(xs, 0, s_x)
            load_piece(0)
            load_piece(1)
            pool.memset(ident[:, :], 0.0).then_inc(s_setup, 1)
            pool.memset(sel[:, :, :], 0.0).then_inc(s_setup, 1)
            pool.wait_ge(s_setup, 2)
            pool.affine_select(out=ident[:, :], in_=ident[:, :], compare_op=ALU.not_equal, fill=1.0,
                               base=0, pattern=[[-1, 128]], channel_multiplier=1).then_inc(s_ident, 1)
            pool.memset(ks[2][:, :, :].rearrange("p a n -> p (a n)").bitcast(u32), 0).then_inc(s_slot2, 1)
            sel_e = sel[:, :, :].rearrange("p c (a h) -> p (c a) h", h=HE)
            for n, base in enumerate((0, -E)):
                pool.affine_select(out=sel_e, in_=sel_e, compare_op=ALU.not_equal, fill=1.0, base=base,
                                   pattern=[[-1, E], [0, HE]], channel_multiplier=1).then_inc(s_setup, 1)
                pool.wait_ge(s_setup, 3 + n)
            for n in range(len(PIECES)):
                high, low = split_target(*PIECES[n])
                pool.wait_ge(s_raw[n % 2], 16 * (n // 2 + 1))
                pool.tensor_scalar(raw[n % 2], raw[n % 2], SW, 1.0, ALU.mult, ALU.mult).then_inc(s_wstep, 1)
                pool.wait_ge(s_wstep, 3 * n + 1)
                pool.tensor_scalar(high, raw[n % 2], 1.0, 1.0, ALU.mult, ALU.mult).then_inc(s_wstep, 1)
                pool.wait_ge(s_wstep, 3 * n + 2)
                pool.tensor_tensor(low, raw[n % 2], high, ALU.subtract).then_inc(s_wstep, 1)
                pool.wait_ge(s_wstep, 3 * n + 3)
                if n + 2 < len(PIECES):
                    load_piece(n + 2)

            load_x(y, 0, s_xr)

            def apart(signal, value):
                if not isinstance(value, int):
                    value = pool.to_reg(value)
                    pool.wait_ge(s_init, SETUP_DVE)
                pool.wait_ge(signal, value)

            def batch(b, more):
                pool.wait_ge(s_bo, 1)
                pool.wait_ge(s_xr, b * 16 + 16)
                pool.tensor_tensor(y[:, :, :], y[:, :, :], bo[:, :].unsqueeze(1).to_broadcast([128, NB, D]),
                                   ALU.add).then_inc(s_xb, 1)
                pool.wait_ge(s_y, b * NB + NB)
                pool.wait_ge(s_yt, b * 4 + 4)
                pool.tensor_tensor(y[:, :, :], y[:, :, :], sb2s[:, :].unsqueeze(1).to_broadcast([128, NB, D]),
                                   ALU.add).then_inc(s_yb, 1)
                if more:
                    apart(s_gt, b * 2 + 2)
                    load_x(xs, b + 1, s_x)
                    apart(s_out, (b + 1) * NG * 16)
                    load_x(y, b + 1, s_xr)

            pool.wait_ge(s_init, SETUP_DVE)
            with pool.Fori(0, B - 1) as b:
                batch(b, True)
            batch(B - 1, False)

        @block.scalar
        def _(act):
            def high_parts(dst, src_ready, base, done, scale):
                for n in range(4):
                    k, half = n % 2, n // 2
                    act.wait_ge(src_ready, base + n + 1)
                    act.activation(dst[:, k, 512 * half:512 * half + 512], ps[:, n, :], ACT.Copy, scale=scale)\
                       .then_inc(done, 1)

            first_weights(act, 1)
            act.dma_start(wraw[:, 6:8, :], w_out.rearrange("(c p) d -> p c d", p=128)).then_inc(s_first, 16)
            act.dma_start(browraw[NC + 4:NC + 6, :], b_qkv[2 * D:3 * D].rearrange("(k p) -> k p", p=128))\
               .then_inc(s_first, 16)
            act.dma_start(bo[:, :], b_out.partition_broadcast(128)).then_inc(s_first, 16)
            high_parts(wth, s_wt, 0, s_wth, SW)
            act.wait_ge(s_wt, 5)
            for k in range(3):
                cols = slice((0, NC, NC + 4)[k], (NC, NC + 4, NC + 6)[k])
                act.activation(bcol[:, cols], ps[:, 4, cols], ACT.Copy, scale=(1.0, SQ, SX)[k]).then_inc(s_bias, 1)
            act.wait_ge(s_bias, 3)
            act.wait_ge(s_init, 2 * NSLOT + 1)
            for k in range(KD):
                act.activation(reph[:, k, :], zero[:, :], ACT.Identity, bias=bcol[:, NC + 4 + k:NC + 5 + k])\
                   .then_inc(s_rep, 1)

            def front(b):
                high_parts(tokh, s_xt, b * 4, s_xh, SX)
                for n in range(8):
                    j = (2, 2, 3, 3, 0, 0, 1, 1)[n]
                    act.wait_ge(s_prj, b * 12 + n + 1)
                    if n >= 2:
                        act.wait_ge(s_qkl, b * 8 + n - 1)
                    act.activation(proj[n % 2], ps[:, 4 + n % 4, :], ACT.Identity,
                                   bias=bcol[:, NC + j:NC + j + 1], scale=SQ / (SX * SW)).then_inc(s_q32, 1)

            def normalized(dst, first, last, done):
                for t in range(first, last):
                    act.activation(dst[:, t, :], dst[:, t, :], ACT.Identity, bias=nmr[:, t:t + 1],
                                   scale=rstd[:, t:t + 1]).then_inc(done, 1)

            def second_norm(b):
                act.wait_ge(s_var2, b + 1)
                act.activation(std[:, :], mv[:, :, 1], ACT.Sqrt).then_inc(s_std2, 1)
                act.wait_ge(s_nm2, b + 1)
                normalized(y, 0, NB, s_n2)

            def rest(b, more):
                for n in range(4):
                    act.wait_ge(s_prj, b * 12 + 8 + n + 1)
                    act.activation(vs[:, 2 * n:2 * n + 2, :, 0:HD].rearrange("p t h d -> p (t h) d"),
                                   ps[:, 4 + n, :].rearrange("p (a d) -> p a d", d=HD), ACT.Copy,
                                   scale=1.0 / (SX * SW)).then_inc(s_v, 1)
                for it in range(NQ + 1):
                    def rows():
                        act.wait_ge(s_ring, b * RING + ring_after_rows(it))
                        if it >= 1:
                            p = it - 1
                            act.wait_ge(s_row[SLOT[p]], (b * PERB[SLOT[p]] + BEFORE[p] + 1) * 16 * ROW_DMAS)
                        act.activation(mrh[:, :], ps[0:32, (ring_after_rows(it) - 1) % 2, 0:TB], ACT.Copy,
                                       scale=-1.0 / SROW).then_inc(s_mrh, 1)

                    if it == 0:
                        rows()
                    if it >= 1:
                        for s in range(STEPS):
                            if it < NQ and s == ROWS_AT - LEAD:
                                rows()
                            n = (it - 1) * STEPS + s
                            u, hp = s // 2, s % 2
                            unit = (it - 1) * NU + u
                            w = 512 if UNITS[u] is None else 256 * len(UNITS[u])
                            act.wait_ge(s_st, b * NQ * STEPS + n + 1)
                            if unit >= 2:
                                act.wait_ge(s_pv, b * NQ * NU + unit - 1)
                            act.activation(pt[unit % 2][:, 2 * hp:2 * hp + 2, 0:w],
                                           ps[:, 2 + 2 * (n % 2):4 + 2 * (n % 2), 0:w], ACT.Exp,
                                           scale=HD**-0.5 / SQ**2).then_inc(s_exp, 1)
                        act.wait_ge(s_pv, b * NQ * NU + it * NU)
                        act.activation(oacc.rearrange("p (a n) -> p a n", a=2), ps[:, OUT0:OUT0 + 2, :],
                                       ACT.Copy).then_inc(s_oacc, 1)
                for half in range(2):
                    act.wait_ge(s_at, b * 2 + half + 1)
                    act.activation(ath[:, 1, 512 * half:512 * half + 512], ps[:, 2 + half, :], ACT.Copy, scale=SX)\
                       .then_inc(s_ah, 1)
                for half in range(2):
                    act.wait_ge(s_var, b * 2 + half + 1)
                    act.activation(std[:, 4 * half:4 * half + 4], mv[:, 4 * half:4 * half + 4, 1], ACT.Sqrt)\
                       .then_inc(s_std, 1)
                    act.wait_ge(s_nm, b * 2 + half + 1)
                    normalized(y, 4 * half, 4 * half + 4, s_y)
                high_parts(tokh, s_yt, b * 4, s_yh, SX)
                act.wait_ge(s_rt, b * NR_ROUTER + 3)
                act.activation(lg[:, :, :], lg[:, :, :], ACT.Exp).then_inc(s_e, 1)

                def gate_parts():
                    for n in range(2):
                        act.wait_ge(s_gt, b * 2 + n + 1)
                        act.activation(cwt[:, 512 * n:512 * n + 512], ps[:, 4 + n, :], ACT.Copy, scale=SC)\
                           .then_inc(s_cwh, 1)

                def silu(g, c, j):
                    fi = b * NG + g
                    act.wait_ge(s_u, fi * NC + c + 1)
                    if isinstance(c, int) and 2 <= c < NS + 2:
                        act.wait_ge(s_hl, fi * NC + c - 1)
                    elif not isinstance(c, int) or c >= NS + 2:
                        act.wait_ge(s_hc, fi * NR + c - NS - 1)
                    elif g > 0:
                        act.wait_ge(s_hc, fi * NR + c - 1)
                    bias = bcol[:, c:c + 1] if isinstance(c, int) else bcol[:, bass.ds(c, 1)]
                    act.activation(hs_[j % 2], ps[:, j % 2, :], ACT.Silu, bias=bias,
                                   scale=1.0 / (SX * SW)).then_inc(s_silu, 1)

                def high(g, c, j):
                    fi = b * NG + g
                    routed = not isinstance(c, int) or c >= NS
                    if routed:
                        act.wait_ge(s_hc, fi * NR + c - NS + 1)
                    if not isinstance(c, int) or c >= 4 or g > 0:
                        act.wait_ge(s_dn, fi * NC + c - 3)
                    if routed:
                        act.activation(hh[j % 4], hc[j % 4], ACT.Copy).then_inc(s_hh, 1)
                    else:
                        act.wait_ge(s_silu, fi * NC + c + 1)
                        act.activation(hh[j % 4], hs_[j % 2], ACT.Copy, scale=SC).then_inc(s_hh, 1)

                silu(0, 0, 0)
                for g in range(NG):
                    for c in range(NS + 4):
                        if g == 0 and c == GATES_AT:
                            gate_parts()
                        silu(g, c + 1, c + 1)
                        high(g, c, c)
                    with act.Fori(NS // 4 + 1, NC // 4 - 1) as it:
                        for j in range(4):
                            silu(g, it * 4 + j + 1, j + 1)
                            high(g, it * 4 + j, j)
                    for c in range(NC - 4, NC):
                        if c + 1 < NC:
                            silu(g, c + 1, c + 1)
                        elif g + 1 < NG:
                            silu(g + 1, 0, 0)
                        high(g, c, c)

            front(0)
            with act.Fori(0, B - 1) as b:
                rest(b, True)
                front(b + 1)
                second_norm(b)
            rest(B - 1, False)
            second_norm(B - 1)

        @block.vector
        def _(dve):
            steps = [0]

            def init(ins):
                steps[0] += 1
                ins.then_inc(s_init, 1)

            def apart(signal, value):
                if not isinstance(value, int):
                    value = dve.to_reg(value)
                    dve.wait_ge(s_init, SETUP_DVE)
                dve.wait_ge(signal, value)

            def low_parts(dst, high, high_done, base, done, scale):
                for n in range(4):
                    k, half = n % 2, n // 2
                    cols = slice(512 * half, 512 * half + 512)
                    dve.wait_ge(high_done, base + n + 1)
                    dve.scalar_tensor_tensor(dst[:, k, cols], ps[:, n, :], scale, high[:, k, cols],
                                             ALU.mult, ALU.subtract).then_inc(done, 1)

            init(dve.memset(zero[:, :], 0.0))
            init(dve.memset(srow[:, :], SROW))
            for s in range(NSLOT):
                init(dve.memset(qs[s][:, :, :].rearrange("p a n -> p (a n)").bitcast(u32), 0))
                if s < NSLOT - 1:
                    init(dve.memset(ks[s][:, :, :].rearrange("p a n -> p (a n)").bitcast(u32), 0))
            assert steps[0] == 2 * NSLOT + 1
            low_parts(wtl, wth, s_wth, 0, s_wtl, SW)
            dve.wait_ge(s_rep, KD)
            for k in range(KD):
                dve.scalar_tensor_tensor(repl[:, k, :], zero[:, :], bcol[:, NC + 4 + k:NC + 5 + k], reph[:, k, :],
                                         ALU.add, ALU.subtract).then_inc(s_rep, 1)
            dve.memset(ps[:, OUT0:OUT0 + 2, :], 0.0).then_inc(s_ofree, 1)
            dve.wait_ge(s_first, FIRST)
            dve.wait_ge(s_bvo, 1)
            dve.scalar_tensor_tensor(bo[:, :], ps[:, 5, 0:D], 1.0 / (SX * SW), bo[:, :], ALU.mult, ALU.add)\
               .then_inc(s_bo, 1)

            def front(b):
                low_parts(tokl, tokh, s_xh, b * 4, s_xl, SX)
                for n in range(8):
                    c, half = (n // 2) % 2, n % 2
                    high, low = (kh, kl) if n < 4 else (qh, ql)
                    cols = slice(512 * half, 512 * half + 512)
                    dve.wait_ge(s_q32, b * 8 + n + 1)
                    dve.tensor_copy(high[:, c, cols], proj[n % 2]).then_inc(s_qkh, 1)
                    dve.wait_ge(s_qkh, b * 8 + n + 1)
                    dve.tensor_tensor(low[:, c, cols], proj[n % 2], high[:, c, cols], ALU.subtract)\
                       .then_inc(s_qkl, 1)

            def norm_stats(first, last, b, ready, stats, aggregated):
                for t in range(first, last):
                    ready(t)
                    dve.bn_stats(bst[:, t, :], y[:, t, :]).then_inc(stats, 1)
                for t in range(first, last):
                    apart(stats, b * NB + t + 1)
                    dve.bn_aggr(mv[:, t, :], bst[:, t, :]).then_inc(aggregated, 1)

            def norm_variance(first, last, aggregated, count, var):
                dve.wait_ge(aggregated, count)
                dve.tensor_scalar(mv[:, first:last, 1], mv[:, first:last, 1], EPS, None, ALU.add).then_inc(var, 1)

            def norm_scale(first, last, b, std_ready, recip, shift):
                dve.wait_ge(std_ready, b + 1)
                dve.reciprocal(rstd[:, first:last], std[:, first:last]).then_inc(recip, 1)
                dve.wait_ge(recip, b + 1)
                dve.scalar_tensor_tensor(nmr[:, first:last], mv[:, first:last, 0], -1.0, rstd[:, first:last],
                                         ALU.mult, ALU.mult).then_inc(shift, 1)

            def second_stats(b, g):
                def ready(t):
                    if t % GB < GB - 1:
                        apart(s_z2, (b * NG + g) * (GB - 1) + t % GB + 1)
                    else:
                        apart(s_ofree, b * NG + g + 2)
                norm_stats(g * GB, g * GB + GB, b, ready, s_bs2, s_ba2)

            def second_norm(b):
                second_stats(b, NG - 1)
                norm_variance(0, NB, s_ba2, b * NB + NB, s_var2)
                norm_scale(0, NB, b, s_std2, s_rstd2, s_nm2)

            front(0)
            dve.wait_ge(s_small, SMALL)
            init(dve.memset(vs[:, :, :, :].rearrange("p t h d -> p (t h) d")[:, :, HD:HD + 1], 1.0))
            init(dve.tensor_tensor(sb2s[:, :], sb2s[:, :], sbraw, ALU.add))
            init(dve.tensor_scalar(rwh[:, :, :], rraw, SW, None, ALU.mult))
            init(dve.tensor_scalar(b2h[:, :], b2raw, SW, None, ALU.mult))
            dve.wait_ge(s_init, steps[0])
            init(dve.scalar_tensor_tensor(rwl[:, :, :], rraw, SW, rwh[:, :, :], ALU.mult, ALU.subtract))
            init(dve.scalar_tensor_tensor(b2l[:, :], b2raw, SW, b2h[:, :], ALU.mult, ALU.subtract))
            assert steps[0] == SETUP_DVE

            def rest(b):
                ring = 0

                def normalize(q, half):
                    o = ps[:, ring % 2, :].rearrange("p (t g d) -> p t g d", t=4, g=4)
                    n = 2 * q + half
                    dve.wait_ge(s_ring, b * RING + ring + 1)
                    dve.reciprocal(rc[:, half, :, :], o[:, :, :, HD]).then_inc(s_rc, 1)
                    dve.wait_ge(s_rc, b * 2 * NQ + n + 1)
                    dve.tensor_tensor(
                        att[:, 4 * half:4 * half + 4, 64 * q:64 * q + 64].rearrange("p t (g d) -> p t g d", g=4),
                        o[:, :, :, 0:HD], rc[:, half, :, :].unsqueeze(3).to_broadcast([128, 4, 4, HD]),
                        ALU.mult).then_inc(s_free, 1)

                for it in range(NQ + 1):
                    for s in range(STEPS):
                        if it < NQ:
                            for m in (2 * s, 2 * s + 1):
                                pos, u = m // NU, m % NU
                                dve.wait_ge(s_ring, b * RING + ring + 1)
                                if UNITS[u] is None:
                                    dst, src = mxp[:, pos, u:u + 1], ps[:, ring % 2, :]
                                else:
                                    k = len(UNITS[u])
                                    dst = mx[:, pos, UNITS[u][0]:UNITS[u][0] + k]
                                    src = ps[:, ring % 2, 0:256 * k].rearrange("p (a n) -> p a n", n=256)
                                dve.reduce_max(dst, src, axis=AX.X).then_inc(s_free, 1)
                                ring += 1
                        if s == 1 and it >= 2:
                            for half in range(2):
                                normalize(it - 2, half)
                                ring += 1
                        if s == 3 and it == NQ:
                            for half in range(2):
                                cols = slice(512 * half, 512 * half + 512)
                                dve.wait_ge(s_ring, b * RING + ring + 1)
                                dve.tensor_scalar(ath[:, 0, cols], ps[:, ring % 2, :], SX, None, ALU.mult)\
                                   .then_inc(s_a0, 1)
                                dve.wait_ge(s_a0, b * 2 + half + 1)
                                dve.scalar_tensor_tensor(atl[:, 0, cols], ps[:, ring % 2, :], SX, ath[:, 0, cols],
                                                         ALU.mult, ALU.subtract).then_inc(s_free, 1)
                                ring += 1
                    if it < NQ:
                        dve.wait_ge(s_free, b * RING + ring)
                        dve.tensor_reduce(mx[:, :, 0:1].rearrange("p g o -> p (g o)"), mxp[:, :, :],
                                          axis=AX.X, op=ALU.max).then_inc(s_mx, 1)
                        dve.wait_ge(s_mrh, b * NQ + it + 1)
                        dve.scalar_tensor_tensor(mrl[:, :], ps[0:32, ring % 2, 0:TB], -1.0 / SROW, mrh[:, :],
                                                 ALU.mult, ALU.subtract).then_inc(s_free, 1)
                        ring += 1
                        assert ring == ring_after_rows(it)
                for half in range(2):
                    normalize(NQ - 1, half)
                    ring += 1
                assert ring == RING

                for half in range(2):
                    cols = slice(512 * half, 512 * half + 512)
                    dve.wait_ge(s_ah, b * 2 + half + 1)
                    dve.scalar_tensor_tensor(atl[:, 1, cols], ps[:, 2 + half, :], SX, ath[:, 1, cols],
                                             ALU.mult, ALU.subtract).then_inc(s_al, 1)
                dve.wait_ge(s_xb, b + 1)
                for half in range(2):
                    for t in range(4 * half, 4 * half + 4):
                        dve.wait_ge(s_op, b * 4 + t // 2 + 1)
                        dve.scalar_tensor_tensor(y[:, t, :], ps[:, 4 + t // 2, 256 * (t % 2):256 * (t % 2) + 256],
                                                 1.0 / (SX * SW), y[:, t, :], ALU.mult, ALU.add)\
                           .then_inc(s_z, 1)
                    norm_stats(4 * half, 4 * half + 4, b, lambda t: dve.wait_ge(s_z, b * NB + t + 1),
                               s_bs, s_ba)
                    norm_variance(4 * half, 4 * half + 4, s_ba, b * NB + 4 * half + 4, s_var)
                for half in range(2):
                    norm_scale(4 * half, 4 * half + 4, b * 2 + half, s_std, s_rstd, s_nm)
                low_parts(tokl, tokh, s_yh, b * 4, s_yl, SX)

                def gated(g, c, j):
                    fi = b * NG + g
                    dve.wait_ge(s_silu, fi * NC + c + 1)
                    dve.wait_ge(s_cwb, fi * NR + c - NS + 1)
                    dve.tensor_tensor(hc[j % 4], hs_[j % 2], ps[:, 2 + j % 2, :], ALU.mult).then_inc(s_hc, 1)

                def low(g, c, j):
                    dve.wait_ge(s_hh, (b * NG + g) * NC + c + 1)
                    if not isinstance(c, int) or c >= NS:
                        dve.tensor_tensor(hl[j % 4], hc[j % 4], hh[j % 4], ALU.subtract).then_inc(s_hl, 1)
                    else:
                        dve.scalar_tensor_tensor(hl[j % 4], hs_[j % 2], SC, hh[j % 4],
                                                 ALU.mult, ALU.subtract).then_inc(s_hl, 1)

                dve.wait_ge(s_lg, b + 1)
                dve.scalar_tensor_tensor(lg[:, :, :], ps[:, 4, :].rearrange("p (t e) -> p t e", e=E),
                                         1.0 / (SX * SW), rb[:, :].unsqueeze(1).to_broadcast([128, NB, E]),
                                         ALU.mult, ALU.add).then_inc(s_rt, 1)
                dve.wait_ge(s_rt, b * NR_ROUTER + 1)
                dve.reduce_max(rmax[:, :], lg[:, :, :], axis=AX.X).then_inc(s_rt, 1)
                dve.wait_ge(s_rt, b * NR_ROUTER + 2)
                dve.tensor_tensor(lg[:, :, :], lg[:, :, :], rmax[:, :].unsqueeze(2).to_broadcast([128, NB, E]),
                                  ALU.subtract).then_inc(s_rt, 1)
                apart(s_e, b + 1)
                for t in range(NB):
                    dve.max(top[:, t, :], lg[:, t, :]).then_inc(s_top, 1)
                low(0, 0, 0)
                apart(s_top, b * 2 * NB + NB)
                for t in range(NB):
                    dve.match_replace(untop[:, t, :], top[:, t, :], lg[:, t, :], -1.0).then_inc(s_top, 1)
                dve.tensor_reduce(nsum[:, :], top[:, :, :], axis=AX.X, op=ALU.add, negate=True)\
                   .then_inc(s_rt, 1)
                low(0, 1, 1)
                dve.wait_ge(s_top, b * 2 * NB + 2 * NB)
                dve.wait_ge(s_rt, b * NR_ROUTER + 4)
                dve.reciprocal(nsum[:, :], nsum[:, :]).then_inc(s_rt, 1)
                dve.scalar_tensor_tensor(untop[:, :, :], untop[:, :, :], 0.0, lg[:, :, :],
                                         ALU.max, ALU.subtract).then_inc(s_rt, 1)
                low(0, 2, 2)
                dve.wait_ge(s_rt, b * NR_ROUTER + 6)
                for n in range(2):
                    dve.tensor_tensor(gate[:, :, E * n:E * n + E], untop[:, :, :],
                                      nsum[:, :].unsqueeze(2).to_broadcast([128, NB, E]), ALU.mult)\
                       .then_inc(s_gate, 1)
                low(0, 3, 3)
                for n in range(2):
                    cols = slice(512 * n, 512 * n + 512)
                    dve.wait_ge(s_cwh, b * 2 + n + 1)
                    dve.scalar_tensor_tensor(cwt[E:2 * E, cols], ps[E:2 * E, 4 + n, :], SC, cwt[E:2 * E, cols],
                                             ALU.mult, ALU.subtract).then_inc(s_cwl, 1)

                for g in range(NG):
                    for c in range(NS):
                        if c == NS - 1:
                            gated(g, NS, NS)
                        if g > 0 or c >= GATES_AT:
                            low(g, c, c)
                        if g > 0 and c == NS // 2:
                            second_stats(b, g - 1)
                    with dve.Fori(NS // 4, NC // 4 - 1) as it:
                        for j in range(4):
                            gated(g, it * 4 + j + 1, j + 1)
                            low(g, it * 4 + j, j)
                    for c in range(NC - 4, NC):
                        if c + 1 < NC:
                            gated(g, c + 1, c + 1)
                        low(g, c, c)
                    if g == 0:
                        dve.wait_ge(s_yb, b + 1)
                    dve.wait_ge(s_dn, (b * NG + g + 1) * NC)
                    for t in range(GB):
                        z = dve.scalar_tensor_tensor(
                            y[:, g * GB + t, :], ps[:, OUT0 + t // 2, 256 * (t % 2):256 * (t % 2) + 256],
                            1.0 / (SC * SW), y[:, g * GB + t, :], ALU.mult, ALU.add)
                        z.then_inc(s_z2 if t < GB - 1 else s_ofree, 1)

            with dve.Fori(0, B - 1) as b:
                rest(b)
                front(b + 1)
                second_norm(b)
            rest(B - 1)
            second_norm(B - 1)

        @block.tensor
        def _(pe):
            def transposed(src, done):
                for n in range(4):
                    k, half = n % 2, n // 2
                    for t in range(4):
                        last = pe.transpose(ps[:, n, 128 * t:128 * t + 128],
                                            src[:, 4 * half + t, 128 * k:128 * k + 128], ident[:, :])
                    last.then_inc(done, 1)

            def parts(dst, stationary, moving, start=True, stop=True, skip=False):
                terms = [(s, m) for k in range(len(stationary[0]))
                         for s, m in ((stationary[0][k], moving[0][k]), (stationary[0][k], moving[1][k]),
                                      (stationary[1][k], moving[0][k]))]
                for n, (s, m) in enumerate(terms):
                    last = pe.matmul(dst, s, m, start=start and n == 0, stop=stop and n == len(terms) - 1,
                                     skip_group_check=skip)
                return last

            pe.wait_ge(s_ident, 1)
            pe.wait_ge(s_first, FIRST)
            transposed(wraw, s_wt)
            pe.transpose(ps[:, 4, 0:NC + 6], browraw, ident[0:NC + 6, 0:NC + 6]).then_inc(s_wt, 1)
            pe.wait_ge(s_wtl, 4)

            def front(b):
                pe.wait_ge(s_x, b * 16 + 16)
                transposed(xs, s_xt)

            def projections(b):
                pe.wait_ge(s_xl, b * 4 + 4)
                for n in range(8):
                    j = (2, 2, 3, 3, 0, 0, 1, 1)[n]
                    half = n % 2
                    if n >= 4:
                        pe.wait_ge(s_q32, b * 8 + n - 3)
                    cols = slice(512 * half, 512 * half + 512)
                    parts(ps[:, 4 + n % 4, :],
                          [[w[:, k, 128 * j:128 * j + 128] for k in range(KD)] for w in (wth, wtl)],
                          [[m[:, k, cols] for k in range(KD)] for m in (tokh, tokl)]).then_inc(s_prj, 1)

            def rest(b, more):
                def value_block(t):
                    if t == 0:
                        pe.wait_ge(s_q32, b * 8 + 8)
                    toks = slice(TB * t, TB * t + TB)
                    last = parts(ps[:, 4 + t // 2, 256 * (t % 2):256 * (t % 2) + 256],
                                 [[m[:, k, toks] for k in range(KD)] for m in (tokh, tokl)],
                                 [[w[:, k, 512:768] for k in range(KD)] for w in (wth, wtl)])
                    if t % 2:
                        last.then_inc(s_prj, 1)

                ring = 0

                def maxima_unit(q, m):
                    pos, u = m // NU, m % NU
                    pr = place(pos)[1]
                    slot = SLOT[q]
                    if ring >= 2:
                        pe.wait_ge(s_free, b * RING + ring - 1)
                    bank = ring % 2
                    if UNITS[u] is None:
                        last = pe.matmul(ps[:, bank, :], qs[slot][:, pr, 0:TB],
                                         ks[slot][:, pos, 512 * u:512 * u + 512], start=True, stop=True)
                    else:
                        for n, i in enumerate(UNITS[u]):
                            last = pe.matmul(ps[:, bank, 256 * n:256 * n + 256],
                                             qs[slot][:, pr, TB * i:TB * i + TB],
                                             blocks(ks[slot][:, pos, :], i), start=True, stop=True)
                    last.then_inc(s_ring, 1)

                def rows(q):
                    pe.wait_ge(s_mx, b * NQ + q + 1)
                    pe.wait_ge(s_free, b * RING + ring - 1)
                    pe.transpose(ps[0:32, ring % 2, 0:TB], mx[:, :, :].rearrange("p g t -> p (g t)"),
                                 ident[:, :]).then_inc(s_ring, 1)

                def scores(q, s):
                    n = q * STEPS + s
                    u, hp = s // 2, s % 2
                    slot = SLOT[q]
                    if n >= 2:
                        pe.wait_ge(s_exp, b * NQ * STEPS + n - 1)
                    for a in range(2):
                        pos = 2 * hp + a
                        pr = place(pos)[1]
                        bank = 2 + 2 * (n % 2) + a
                        if UNITS[u] is None:
                            last = pe.matmul(ps[:, bank, :], ks[slot][:, pos, 0:TB],
                                             qs[slot][:, pr, 512 * u:512 * u + 512], start=True, stop=True)
                        else:
                            for m, i in enumerate(UNITS[u]):
                                last = pe.matmul(ps[:, bank, 256 * m:256 * m + 256],
                                                 ks[slot][:, pos, TB * i:TB * i + TB],
                                                 blocks(qs[slot][:, pr, :], i), start=True, stop=True)
                    last.then_inc(s_st, 1)

                def sum_values(q, u):
                    unit = q * NU + u
                    pe.wait_ge(s_exp, b * NQ * STEPS + q * STEPS + 2 * u + 2)
                    if u == 0 and q >= 1:
                        pe.wait_ge(s_oacc, b * NQ + q)
                    end = u == NU - 1
                    products = []
                    if UNITS[u] is None:
                        products.append((0, OUT0 + u, slice(0, 512), slice(0, 512), True, False))
                    else:
                        for m, i in enumerate(UNITS[u]):
                            bank, col = OUT0 + i // 4, TB * (i % 4)
                            products.append((i, OUT0, slice(0, TB), slice(256 * m, 256 * m + TB), False, end))
                            products.append((i, bank, slice(col, col + TB),
                                             slice(256 * m + TB, 256 * m + 256), False, end))
                    for i, bank, dst, src, start, stop in products:
                        for g in range(4):
                            pos = 2 * (g % 2) + g // 2
                            last = pe.matmul(ps[32 * g:32 * g + HD + 1, bank, dst], vs[:, i, 4 * q + g, :],
                                             pt[unit % 2][:, pos, src], start=start, stop=stop,
                                             skip_group_check=True)
                    last.then_inc(s_pv, 1)

                def output_back(q):
                    nonlocal ring
                    pe.wait_ge(s_oacc, b * NQ + q + 1)
                    for half in range(2):
                        pe.wait_ge(s_free, b * RING + ring - 1)
                        for t in range(4):
                            cols = slice(TB * (4 * half + t), TB * (4 * half + t) + TB)
                            last = pe.transpose(ps[:, ring % 2, TB * t:TB * t + TB], oacc[:, cols], ident[:, :])
                        last.then_inc(s_ring, 1)
                        ring += 1

                for it in range(NQ + 1):
                    for s in range(STEPS + LEAD):
                        if it < NQ and s < STEPS:
                            if s == 0:
                                pe.wait_ge(s_stk[SLOT[it]],
                                           (b * PERB[SLOT[it]] + BEFORE[it] + 1) * 16 * STACK_DMAS)
                            maxima_unit(it, 2 * s)
                            ring += 1
                            maxima_unit(it, 2 * s + 1)
                            ring += 1
                        if it == 0 and s < NB:
                            value_block(s)
                        if 0 < it < NQ and s == ROWS_AT:
                            rows(it)
                            ring += 1
                        if s == 1 and it >= 2:
                            output_back(it - 2)
                        if s == 3 and it == NQ:
                            for half in range(2):
                                pe.wait_ge(s_free, b * RING + ring - 1)
                                for t in range(4):
                                    last = pe.transpose(ps[:, ring % 2, TB * t:TB * t + TB],
                                                        att[:, 4 * half + t, 0:128], ident[:, :])
                                last.then_inc(s_ring, 1)
                                ring += 1
                        if it >= 1 and s >= LEAD:
                            q, r = it - 1, s - LEAD
                            if r == 0:
                                if q == 0:
                                    pe.wait_ge(s_v, b * 4 + 4)
                                pe.wait_ge(s_row[SLOT[q]],
                                           (b * PERB[SLOT[q]] + BEFORE[q] + 1) * 16 * ROW_DMAS)
                            scores(q, r)
                            if r % 2 and r >= 3:
                                sum_values(q, (r - 3) // 2)
                    if it == 0:
                        rows(it)
                        ring += 1
                    if it >= 1:
                        sum_values(it - 1, NU - 1)
                output_back(NQ - 1)
                assert ring == RING

                pe.wait_ge(s_free, b * RING + RING)
                for half in range(2):
                    for t in range(4):
                        last = pe.transpose(ps[:, 2 + half, TB * t:TB * t + TB], att[:, 4 * half + t, 128:256],
                                            ident[:, :])
                    last.then_inc(s_at, 1)
                for t in range(NB):
                    pe.wait_ge(s_al, b * 2 + t // 4 + 1)
                    toks = slice(TB * t, TB * t + TB)
                    last = parts(ps[:, 4 + t // 2, 256 * (t % 2):256 * (t % 2) + 256],
                                 [[m[:, k, toks] for k in range(KD)] for m in (ath, atl)],
                                 [[w[:, k, 768:1024] for k in range(KD)] for w in (wth, wtl)])
                    if t % 2:
                        last.then_inc(s_op, 1)

                for n in range(4):
                    k, half = n % 2, n // 2
                    for t in range(4 * half, 4 * half + 4):
                        pe.wait_ge(s_y, b * NB + t + 1)
                        last = pe.transpose(ps[:, n, 128 * (t % 4):128 * (t % 4) + 128],
                                            y[:, t, 128 * k:128 * k + 128], ident[:, :])
                    last.then_inc(s_yt, 1)
                pe.wait_ge(s_init, SETUP_DVE)
                for t in range(NB):
                    toks = slice(TB * t, TB * t + TB)
                    pe.wait_ge(s_yl, b * 4 + 2 * (t // 4) + 2)
                    last = parts(ps[:, 4, E * t:E * t + E],
                                 [[m[:, k, toks] for k in range(KD)] for m in (tokh, tokl)],
                                 [[w[:, k, :] for k in range(KD)] for w in (rwh, rwl)])
                last.then_inc(s_lg, 1)

                def up(g, c, j):
                    cols = slice(128 * c, 128 * c + 128) if isinstance(c, int) else bass.ds(c * 128, 128)
                    toks = slice(GT * g, GT * g + GT)
                    if not isinstance(c, int) or c >= 2 or g > 0:
                        pe.wait_ge(s_silu, (b * NG + g) * NC + c - 1)
                    parts(ps[:, j % 2, :], [[w[:, k, cols] for k in range(KD)] for w in (w1h, w1l)],
                          [[m[:, k, toks] for k in range(KD)] for m in (tokh, tokl)]).then_inc(s_u, 1)

                def spread(g, c, j):
                    if not isinstance(c, int) or c >= NS + 2 or g > 0:
                        pe.wait_ge(s_hc, (b * NG + g) * NR + c - NS - 1)
                    one = sel[:, c - NS, :] if isinstance(c, int) else \
                        sel[:, bass.ds(c - NS, 1), :].rearrange("p o m -> p (o m)")
                    pe.matmul(ps[:, 2 + j % 2, :], one, cwt[:, GT * g:GT * g + GT],
                              start=True, stop=True).then_inc(s_cwb, 1)

                def gated_bias(g):
                    for t in range(GB):
                        toks = cwt[:, GT * g + TB * t:GT * g + TB * t + TB]
                        dst = ps[:, OUT0 + t // 2, 256 * (t % 2):256 * (t % 2) + 256]
                        for part in (b2h, b2l):
                            pe.matmul(dst, toks, part[:, :], start=False, stop=False, skip_group_check=True)

                def down(g, c, j, end=False):
                    first = isinstance(c, int) and c == 0
                    if first:
                        pe.wait_ge(s_ofree, b * NG + g + 1)
                    pe.wait_ge(s_hl, (b * NG + g) * NC + c + 1)
                    for t in range(GB):
                        toks = slice(TB * t, TB * t + TB)
                        if isinstance(c, int):
                            ws = [w[:, c, :] for w in (w2h, w2l)]
                        else:
                            ws = [w[:, bass.ds(c, 1), :].rearrange("p o d -> p (o d)") for w in (w2h, w2l)]
                        last = parts(ps[:, OUT0 + t // 2, 256 * (t % 2):256 * (t % 2) + 256],
                                     [[h[j % 4][:, toks]] for h in (hh, hl)], [[w] for w in ws],
                                     start=first and t % 2 == 0, stop=end, skip=True)
                    last.then_inc(s_dn, 1)

                pe.wait_ge(s_wstep, 3 * len(PIECES))
                pe.wait_ge(s_setup, 4)
                up(0, 0, 0)
                up(0, 1, 1)
                for g in range(NG):
                    for c in range(NS):
                        if g == 0 and c == GATES_AT:
                            pe.wait_ge(s_gate, b * 2 + 2)
                            for n in range(2):
                                for t in range(4):
                                    last = pe.transpose(ps[:, 4 + n, TB * t:TB * t + TB], gate[:, 4 * n + t, :],
                                                        ident[:, :])
                                last.then_inc(s_gt, 1)
                        up(g, c + 2, c)
                        if c + 2 >= NS:
                            if g == 0 and c + 2 == NS:
                                pe.wait_ge(s_cwl, b * 2 + 2)
                            spread(g, c + 2, c)
                        down(g, c, c)
                    gated_bias(g)
                    with pe.Fori(NS // 4, NC // 4 - 1) as it:
                        for j in range(4):
                            up(g, it * 4 + j + 2, j)
                            spread(g, it * 4 + j + 2, j)
                            down(g, it * 4 + j, j)
                    for c in range(NC - 4, NC):
                        if c + 2 < NC:
                            up(g, c + 2, c)
                            spread(g, c + 2, c)
                        elif g + 1 < NG:
                            up(g + 1, c + 2 - NC, c)
                        elif c == NC - 1 and more:
                            pe.wait_ge(s_silu, (b * NG + NG) * NC)
                            pe.wait_ge(s_hc, (b * NG + NG) * NR)
                            front(b + 1)
                        down(g, c, c, c == NC - 1)

            front(0)
            pe.wait_ge(s_rep, 2 * KD)
            parts(ps[:, 5, 0:D], [[m[:, k, :] for k in range(KD)] for m in (reph, repl)],
                  [[w[:, k, 768:1024] for k in range(KD)] for w in (wth, wtl)]).then_inc(s_bvo, 1)
            pe.wait_ge(s_bo, 1)
            projections(0)
            with pe.Fori(0, B - 1) as b:
                rest(b, True)
                projections(b + 1)
            rest(B - 1, False)


_INS = ['L0_attn_x', 'L0_attn_w_qkv', 'L0_attn_b_qkv', 'L0_attn_w_out', 'L0_attn_b_out',
        'L0_ffn_router_w', 'L0_ffn_router_b', 'L0_ffn_w1', 'L0_ffn_b1', 'L0_ffn_w2', 'L0_ffn_b2',
        'L0_ffn_sw1', 'L0_ffn_sb1', 'L0_ffn_sw2', 'L0_ffn_sb2']
_OUTS = [((4, 1024, 256), 'float32')]


def kernel(**inputs):
    import numpy as _np
    import concourse.bacc as _bacc
    from concourse import mybir as _mybir
    from concourse.bass_utils import run_bass_kernel_spmd as _run

    nc = _bacc.Bacc("TRN2", target_bir_lowering=False, num_devices=1)
    arrays, args = {}, []
    for name in _INS:
        a = _np.ascontiguousarray(inputs[name])
        arrays[f"in_{name}_dram"] = a
        args.append(nc.dram_tensor(f"in_{name}_dram", a.shape, _mybir.dt.from_np(a.dtype), kind="ExternalInput").ap())
    for i, (shape, dtype) in enumerate(_OUTS):
        dt = _mybir.dt.from_np(_np.dtype(dtype))
        args.append(nc.dram_tensor(f"out_{i}_dram", shape, dt, kind="ExternalOutput").ap())
    post_ln_block_kernel(nc, *args)
    r = _run(nc, [arrays], core_ids=[0])
    return r.results[0]["out_0_dram"]
```

```python
import concourse.bass as bass
from concourse import mybir
from contextlib import ExitStack


def post_ln_block_kernel(
    nc: bass.Bass,
    x: bass.AP,
    w_qkv: bass.AP,
    b_qkv: bass.AP,
    w_out: bass.AP,
    b_out: bass.AP,
    router_w: bass.AP,
    router_b: bass.AP,
    w1: bass.AP,
    b1: bass.AP,
    w2: bass.AP,
    b2: bass.AP,
    sw1: bass.AP,
    sb1: bass.AP,
    sw2: bass.AP,
    sb2: bass.AP,
    out: bass.AP,
):
    f32, f16, u32 = mybir.dt.float32, mybir.dt.float16, mybir.dt.uint32
    ALU = mybir.AluOpType
    ACT = mybir.ActivationFunctionType
    AX = mybir.AxisListType

    B, L, D = x.shape
    NH, HD = 16, 16
    TB = 128
    NB = L // TB
    KD = D // 128
    E, _, HE = w1.shape
    ES, _, HS = sw1.shape
    NR = E * HE // 128
    NS = ES * HS // 128
    NC = NS + NR
    HID = NC * 128
    TOPK = 8
    NQ = 4
    GT = 512
    NG = L // GT
    GB = GT // TB
    EPS = 1e-5

    SX, SW, SQ, SC = 2.0**6, 2.0**8, 2.0**5, 2.0**4
    SROW = 2.0**10

    UNITS = [None, None] + [list(range(i, min(i + 2, NB))) for i in range(1, NB, 2)]
    NU = len(UNITS)
    SLOT = [0, 1, 2, 0]
    NSLOT = 3
    FIRST_HALF, STACK_DMAS = 10, (9, 10, 10, 10)
    BEFORE = [SLOT[:q].count(SLOT[q]) for q in range(NQ)]
    PERB = [SLOT.count(s) for s in range(NSLOT)]
    ROW_DMAS = 2
    MU = 4 * NU
    STEPS = 2 * NU
    GATES_AT = 4
    LEAD, MAX_STEPS, ROWS_AT = 2, 12, 12
    BACK_AT = 1
    VALUES_FIRST = 5
    K_AHEAD = 2
    STD_AT = 7
    HIGH_BY_ACT = (0, 1, 2, 3)
    SCALE_AT = 7
    XBANK = (4, 5, 0, 1)
    RING = NQ * (MU + 1 + 2) + 2
    FIRST, SMALL = 11 * 16, 7 * 16
    SETUP_DVE = 7 + 2 * NSLOT

    xt = x.rearrange("b (t p) d -> b p t d", p=TB)
    ot = out.rearrange("b (t p) d -> b p t d", p=TB)

    ctx = ExitStack()
    with ctx:
        def sb(name, shape, dt=f32):
            return ctx.enter_context(nc.sbuf_tensor(name, shape, dt))

        def sem(name):
            return ctx.enter_context(nc.semaphore(name))

        y = sb("y", [128, NB, D])
        raw = [y[:, 4 * r:4 * r + 4, :].rearrange("p a d -> p (a d)") for r in range(2)]
        tok = sb("tok", [128, NB * D])
        tokh = tok[:, 0:1024].bitcast(f16).rearrange("p (k n) -> p k n", k=KD)
        tokl = tok[:, 1024:2048].bitcast(f16).rearrange("p (k n) -> p k n", k=KD)
        att = tok[:, :].rearrange("p (t d) -> p t d", t=NB)

        kq = sb("kq", [128, 5120])
        kh = kq[:, 0:1024].bitcast(f16).rearrange("p (c n) -> p c n", c=2)
        kl = kq[:, 1024:2048].bitcast(f16).rearrange("p (c n) -> p c n", c=2)
        qh = kq[:, 2048:3072].bitcast(f16).rearrange("p (c n) -> p c n", c=2)
        ql = kq[:, 3072:4096].bitcast(f16).rearrange("p (c n) -> p c n", c=2)
        proj = [kq[:, 4096 + 512 * r:4608 + 512 * r] for r in range(2)]
        oacc = kq[:, 4096:5120]
        late = oacc
        xs = kq[:, 3072:5120].rearrange("p (t d) -> p t d", t=NB)
        ath = kq[:, 0:1024].bitcast(f16).rearrange("p (k n) -> p k n", k=KD)
        atl = kq[:, 1024:2048].bitcast(f16).rearrange("p (k n) -> p k n", k=KD)
        lg = kq[:, 2048:2560].rearrange("p (t e) -> p t e", t=NB)
        untop = kq[:, 2560:3072].rearrange("p (t e) -> p t e", t=NB)
        gate = kq[:, 3072:4096].rearrange("p (t e) -> p t e", t=NB)

        qs = [sb(f"qs{s}", [128, 2, L], f16) for s in range(NSLOT)]
        ks = [sb(f"ks{s}", [128, 4, L], f16) for s in range(NSLOT)]
        vs = sb("vs", [128, NB, NH, HD + 1])
        work = sb("work", [128, 5120])
        pt = [work[:, 2048 * r:2048 * r + 2048].rearrange("p (g n) -> p g n", g=4) for r in range(2)]
        hs_ = [work[:, 512 * r:512 * r + 512] for r in range(2)]
        hc = [work[:, 1024 + 512 * r:1536 + 512 * r] for r in range(4)]
        hh = [work[:, 3072 + 256 * r:3328 + 256 * r].bitcast(f16) for r in range(4)]
        hl = [work[:, 4096 + 256 * r:4352 + 256 * r].bitcast(f16) for r in range(4)]
        wraw = work[:, 0:2048].rearrange("p (j d) -> p j d", j=8)
        reph = work[:, 0:128].bitcast(f16).rearrange("p (k m) -> p k m", k=KD)
        repl = work[:, 128:256].bitcast(f16).rearrange("p (k m) -> p k m", k=KD)
        rraw = work[:, 2048:2176].rearrange("p (k e) -> p k e", k=KD)
        b2raw = work[:, 2304:2560]
        browraw = work[0:NC + 6, 2560:2688]
        sbraw = work[:, 2688:2944]

        w1h, w1l = sb("w1h", [128, KD, HID], f16), sb("w1l", [128, KD, HID], f16)
        w2h, w2l = sb("w2h", [128, NC, D], f16), sb("w2l", [128, NC, D], f16)
        wth, wtl = sb("wth", [128, KD, 1024], f16), sb("wtl", [128, KD, 1024], f16)
        rwh, rwl = sb("rwh", [128, KD, E], f16), sb("rwl", [128, KD, E], f16)
        b2h, b2l = sb("b2h", [128, D], f16), sb("b2l", [128, D], f16)
        bcol = sb("bcol", [128, NC + 6])
        bo, sb2s = sb("bo", [128, D]), sb("sb2s", [128, D])
        rb = sb("rb", [128, E])
        sel = sb("sel", [128, NR, 128], f16)
        cwt = sb("cwt", [128, L], f16)
        ident = sb("ident", [128, 128])
        zero = sb("zero", [128, 128], f16)
        srow = sb("srow", [128, 128], f16)
        mxp = sb("mxp", [128, 4, 2])
        mx = sb("mx", [128, 4, NB])
        mrh, mrl = sb("mrh", [32, TB], f16), sb("mrl", [32, TB], f16)
        rc = sb("rc", [128, 2, 4, 4])
        bst = sb("bst", [128, NB, 6])
        mv = sb("mv", [128, NB, 2])
        std = sb("std", [128, NB])
        rstd = sb("rstd", [128, NB])
        nmr = sb("nmr", [128, NB])
        rmax = sb("rmax", [128, NB])
        top = sb("top", [128, NB, TOPK])
        nsum = sb("nsum", [128, NB])

        ps = ctx.enter_context(nc.psum_tensor("ps", [128, 8, 512], f32))
        OUT0 = 6

        s_first = sem("projection_weights_loaded")
        s_small = sem("small_weights_loaded")
        s_slot2 = sem("last_slot_zeroed")
        s_rows = sem("constant_rows_loaded")
        s_rep = sem("value_bias_high")
        s_bvo = sem("value_bias_projected")
        s_bo = sem("output_bias_ready")
        s_ident = sem("identity_ready")
        s_setup = sem("pool_setup_steps")
        s_raw = [sem(f"raw_weights_loaded{r}") for r in range(2)]
        s_late = sem("late_raw_weights_loaded")
        s_wstep = sem("weight_split_steps")
        s_wt = sem("weights_transposed")
        s_wth = sem("transposed_weights_high")
        s_wtl = sem("transposed_weights_low")
        s_bias = sem("bias_columns_ready")
        s_init = sem("vector_setup_steps")
        s_x = sem("x_loaded")
        s_xr = sem("x_residual_loaded")
        s_a0 = sem("first_features_high")
        s_xt, s_xh, s_xl = sem("x_transposed"), sem("x_high"), sem("x_low")
        s_prj, s_q32 = sem("projected"), sem("projection_out_of_psum")
        s_qkh, s_qkl, s_v = sem("qk_high_by_scalar"), sem("qk_low"), sem("values_ready")
        s_qkd = sem("qk_high_by_vector")
        s_half = sem("first_half_stacks_loaded")
        s_stk = [sem(f"stacks_loaded{s}") for s in range(NSLOT)]
        s_row = [sem(f"max_rows_loaded{s}") for s in range(NSLOT)]
        s_ring, s_free = sem("ring_filled"), sem("ring_read")
        s_mx = sem("maxima_ready")
        s_mrh = sem("max_rows_high")
        s_st, s_exp = sem("scores_ready"), sem("probabilities_ready")
        s_pv, s_oacc = sem("values_summed"), sem("quad_output_copied")
        s_rc = sem("reciprocal_sums_ready")
        s_at, s_ah, s_al = sem("attention_transposed"), sem("attention_high"), sem("attention_low")
        s_op = sem("output_projected")
        s_xb = sem("residual_ready")
        s_z, s_bs, s_ba = sem("ln1_sum_ready"), sem("ln1_stats"), sem("ln1_mean_var")
        s_var, s_std, s_rstd = sem("ln1_var"), sem("ln1_std"), sem("ln1_rstd")
        s_nm, s_nm2 = sem("ln1_shift"), sem("ln2_shift")
        s_y = sem("ln1_done")
        s_yt, s_yh, s_yl = sem("y_transposed"), sem("y_high"), sem("y_low")
        s_yb = sem("ffn_residual_ready")
        s_lg, s_rt, s_e = sem("logits_ready"), sem("router_steps"), sem("router_exp_done")
        s_gt, s_cwh, s_cwl = sem("gates_transposed"), sem("gates_high"), sem("gates_low")
        s_u, s_cwb = sem("hidden_ready"), sem("gates_spread")
        s_silu, s_hc = sem("silu_done"), sem("hidden_gated")
        s_hh, s_hl = sem("hidden_high"), sem("hidden_low")
        s_dn = sem("down_done")
        s_ofree = sem("output_banks_free")
        s_z2, s_bs2, s_ba2 = sem("ln2_sum_ready"), sem("ln2_stats"), sem("ln2_mean_var")
        s_var2, s_std2, s_rstd2 = sem("ln2_var"), sem("ln2_std"), sem("ln2_rstd")
        s_n2, s_n2v = sem("ln2_done"), sem("ln2_done_by_vector")
        s_yv = sem("ln1_done_by_vector")
        s_out = sem("output_stored")
        s_top, s_gate = sem("top8_steps"), sem("gates_ready")
        NR_ROUTER = 6

        block = ctx.enter_context(nc.Block())

        def blocks(ap, i):
            return ap.rearrange("p (a c) -> p a c", c=TB)[:, 0:i + 1:i, :]

        def place(pos):
            return pos // 2, pos % 2

        def maxima_of(s):
            return range(MU * min(s, MAX_STEPS) // MAX_STEPS, MU * min(s + 1, MAX_STEPS) // MAX_STEPS)

        def stack_loads(b, q):
            mine = [n for p, n in enumerate(STACK_DMAS) if SLOT[p] == SLOT[q]]
            return (b * sum(mine) + sum(mine[:BEFORE[q] + 1])) * 16

        def head_of(m):
            return (0, 2, 1, 3)[m // NU]

        def ring_bank(ring):
            return ring % 4 if ring < MU else ring % 2

        def ring_after_rows(q):
            return (q + 1) * (MU + 1) + 2 * max(0, q - 1)

        w_qk = w_qkv[0:2 * D, :].rearrange("(j t c f) d -> j c t f d", j=2, t=4, c=2)
        b_qk = b_qkv[0:2 * D].rearrange("(j t c f) -> j c t f", j=2, t=4, c=2)

        @block.sync
        def _(sp):
            for n in range(4):
                sp.dma_start(wraw[:, n, :], w_qk[n // 2, n % 2]).then_inc(s_first, 16)
            sp.dma_start(wraw[:, 4:6, :], w_qkv[2 * D:3 * D, :].rearrange("(c p) d -> p c d", p=128))\
              .then_inc(s_first, 16)
            sp.dma_start(browraw[NS:NC, :], b1.rearrange("(c a) h -> c (a h)", a=128 // HE)).then_inc(s_first, 16)
            sp.dma_start(browraw[0:NS, :], sb1.rearrange("e (c h) -> (e c) h", h=128)).then_inc(s_first, 16)
            sp.dma_start(sb2s[:, :], sb2[0, :].partition_broadcast(128)).then_inc(s_small, 16)
            sp.dma_start(sbraw, sb2[1, :].partition_broadcast(128)).then_inc(s_small, 16)
            sp.dma_start(rb[:, :], router_b.partition_broadcast(128)).then_inc(s_small, 16)
            sp.dma_start(rraw, router_w.rearrange("(k p) e -> p k e", p=128)).then_inc(s_small, 16)
            for r in range(2):
                sp.dma_start(b2raw[E * r:E * r + E, :], b2).then_inc(s_small, 16)

            sp.wait_ge(s_init, 2 * NSLOT + 1)
            sp.wait_ge(s_slot2, 1)
            for slot in range(NSLOT):
                for e in range(2):
                    for j in range(2):
                        row = 96 + e + 2 * j
                        sp.dma_start(ks[slot][row:row + 1, 2 * e:2 * e + 2, :]
                                     .rearrange("p a (t c) -> p (a t) c", c=TB),
                                     srow[0:1, :].unsqueeze(1).to_broadcast([1, 2 * NB, TB]))\
                          .then_inc(s_rows, 16)

            def apart(signal, value):
                value = sp.to_reg(value)
                sp.wait_ge(s_init, 2 * NSLOT + 1)
                sp.wait_ge(signal, value)

            def load(part, source, side, rows, index, done):
                sp.dma_start(side[rows, index[0], :], part[source, index[1], :]).then_inc(done, 16)

            def k_loads(q, c0, c1, done):
                return [(part, slice(32 * q + 16 * e, 32 * q + 16 * e + 16), ks[SLOT[q]],
                         slice(32 * r + 16 * e, 32 * r + 16 * e + 16), (slice(2 * e + c0, 2 * e + c1), slice(c0, c1)),
                         done) for e in range(2) for r, part in enumerate((kh, kl, kh))]

            def q_loads(q, c0, c1, done):
                return [(part, slice(32 * q, 32 * q + 32), qs[SLOT[q]], slice(32 * r, 32 * r + 32),
                         (slice(c0, c1), slice(c0, c1)), done) for r, part in enumerate((qh, qh, ql))]

            def no_maxima(q, done):
                sp.dma_start(qs[SLOT[q]][96:100, :, :].rearrange("p a (t c) -> p (a t) c", c=TB),
                             zero[0:4, :].unsqueeze(1).to_broadcast([4, 2 * NB, TB])).then_inc(done, 16)

            def stacks(q):
                for one in k_loads(q, 0, 2, s_stk[SLOT[q]]) + q_loads(q, 0, 2, s_stk[SLOT[q]]):
                    load(*one)

            def front(b):
                for q in range(3):
                    no_maxima(q, s_stk[SLOT[q]] if q else s_half)
                later = k_loads(0, 1, 2, s_stk[0])
                sp.wait_ge(s_qkl, b * 8 + 2)
                for one in k_loads(0, 0, 1, s_half):
                    load(*one)
                sp.wait_ge(s_qkl, b * 8 + 4)
                for one in later[:K_AHEAD]:
                    load(*one)
                sp.wait_ge(s_qkl, b * 8 + 6)
                for one in q_loads(0, 0, 1, s_half):
                    load(*one)
                for one in later[K_AHEAD:]:
                    load(*one)
                sp.wait_ge(s_qkl, b * 8 + 8)
                for one in q_loads(0, 1, 2, s_stk[0]):
                    load(*one)
                stacks(1)
                stacks(2)

            def rest(b):
                for q in range(NQ):
                    apart(s_mrh, b * NQ + q + 1)
                    apart(s_free, b * RING + ring_after_rows(q))
                    slot = SLOT[q]
                    for j, part in enumerate((mrh, mrl)):
                        sp.dma_start(qs[slot][96 + 2 * j:98 + 2 * j, :, :], part[:, :]).then_inc(s_row[slot], 16)
                    if q == 1:
                        sp.wait_ge(s_st, b * NQ * STEPS + STEPS)
                        no_maxima(3, s_stk[SLOT[3]])
                        stacks(3)
                sp.wait_ge(s_st, b * NQ * STEPS + NQ * STEPS)

            def store(b):
                for g in range(NG):
                    sp.wait_ge(s_n2, b * (GB + GB // 2) + (GB, GB + GB // 2)[g])
                    if g == NG - 1:
                        apart(s_n2v, b * (GB // 2) + GB // 2)
                    sp.dma_start(ot[b, :, g * GB:g * GB + GB, :] if isinstance(b, int) else
                                 ot[bass.ds(b, 1), :, g * GB:g * GB + GB, :].rearrange("o p t d -> (o p) t d"),
                                 y[:, g * GB:g * GB + GB, :]).then_inc(s_out, 16)

            front(0)
            with sp.Fori(0, B - 1) as b:
                rest(b)
                front(b + 1)
                store(b)
            rest(B - 1)
            store(B - 1)
            sp.wait_ge(s_rows, 4 * NSLOT * 16)
            sp.wait_ge(s_out, B * NG * 16)

        PIECES = [("w1", k, e0) for k in range(KD) for e0 in range(0, E, 16)]
        PIECES += [("sw1", k, 0) for k in range(KD)]
        PIECES += [("sw2", c, 0) for c in range(0, NS, 4)] + [("w2", c, 0) for c in range(0, NR, 4)]
        LATE = 4
        NOW = len(PIECES) - LATE
        w2r = w2.rearrange("(c a) h d -> (a h) c d", a=128 // HE)
        sw2r = sw2.rearrange("e (c p) d -> p (e c) d", p=128)

        def split_target(kind, i, j):
            if kind == "w1":
                cols = slice(NS * 128 + j * HE, NS * 128 + j * HE + 1024)
                return w1h[:, i, cols], w1l[:, i, cols]
            if kind == "sw1":
                return w1h[:, i, 0:NS * 128], w1l[:, i, 0:NS * 128]
            c = NS + i if kind == "w2" else i
            return (w[:, c:c + 4, :].rearrange("p c d -> p (c d)") for w in (w2h, w2l))

        @block.gpsimd
        def _(pool):
            def load_x(dst, b, done):
                pool.dma_start(dst[:, :, :], xt[b] if isinstance(b, int) else
                               xt[bass.ds(b, 1)].rearrange("o p t d -> (o p) t d")).then_inc(done, 16)

            def load_piece(n, dst, done):
                kind, i, j = PIECES[n]
                if kind == "w1":
                    dst = dst.rearrange("p (e h) -> p e h", h=HE)
                    src = w1[j:j + 16, 128 * i:128 * i + 128, :].rearrange("e p h -> p e h")
                elif kind == "sw1":
                    dst = dst.rearrange("p (e h) -> p e h", h=HS)
                    src = sw1[:, 128 * i:128 * i + 128, :].rearrange("e p h -> p e h")
                else:
                    dst = dst.rearrange("p (c d) -> p c d", d=D)
                    src = (w2r if kind == "w2" else sw2r)[:, i:i + 4, :]
                pool.dma_start(dst, src).then_inc(done, 16)

            def split_piece(n, src):
                high, low = split_target(*PIECES[n])
                pool.tensor_scalar(src, src, SW, 1.0, ALU.mult, ALU.mult).then_inc(s_wstep, 1)
                pool.wait_ge(s_wstep, 3 * n + 1)
                pool.tensor_scalar(high, src, 1.0, 1.0, ALU.mult, ALU.mult).then_inc(s_wstep, 1)
                pool.wait_ge(s_wstep, 3 * n + 2)
                pool.tensor_tensor(low, src, high, ALU.subtract).then_inc(s_wstep, 1)
                pool.wait_ge(s_wstep, 3 * n + 3)

            load_x(xs, 0, s_x)
            pool.memset(ident[:, :], 0.0).then_inc(s_setup, 1)
            pool.memset(sel[:, :, :], 0.0).then_inc(s_setup, 1)
            pool.wait_ge(s_setup, 2)
            pool.affine_select(out=ident[:, :], in_=ident[:, :], compare_op=ALU.not_equal, fill=1.0,
                               base=0, pattern=[[-1, 128]], channel_multiplier=1).then_inc(s_ident, 1)
            pool.memset(ks[2][:, :, :].rearrange("p a n -> p (a n)").bitcast(u32), 0).then_inc(s_slot2, 1)
            sel_e = sel[:, :, :].rearrange("p c (a h) -> p (c a) h", h=HE)
            for n, base in enumerate((0, -E)):
                pool.affine_select(out=sel_e, in_=sel_e, compare_op=ALU.not_equal, fill=1.0, base=base,
                                   pattern=[[-1, E], [0, HE]], channel_multiplier=1).then_inc(s_setup, 1)
                pool.wait_ge(s_setup, 3 + n)
            pool.wait_ge(s_first, FIRST)
            load_piece(0, raw[0], s_raw[0])
            load_piece(1, raw[1], s_raw[1])
            for n in range(NOW):
                pool.wait_ge(s_raw[n % 2], 16 * (n // 2 + 1))
                split_piece(n, raw[n % 2])
                if n + 2 < NOW:
                    load_piece(n + 2, raw[n % 2], s_raw[n % 2])
            load_x(y, 0, s_xr)

            def apart(signal, value):
                if not isinstance(value, int):
                    value = pool.to_reg(value)
                    pool.wait_ge(s_init, SETUP_DVE)
                pool.wait_ge(signal, value)

            def residual(b):
                pool.wait_ge(s_bo, 1)
                pool.wait_ge(s_xr, b * 16 + 16)
                pool.tensor_tensor(y[:, :, :], y[:, :, :], bo[:, :].unsqueeze(1).to_broadcast([128, NB, D]),
                                   ALU.add).then_inc(s_xb, 1)

            def shared_bias(b):
                pool.wait_ge(s_y, b * 4 + 4)
                pool.wait_ge(s_yv, b * 4 + 4)
                pool.wait_ge(s_yt, b * 4 + 4)
                pool.tensor_tensor(y[:, :, :], y[:, :, :], sb2s[:, :].unsqueeze(1).to_broadcast([128, NB, D]),
                                   ALU.add).then_inc(s_yb, 1)

            def next_x(b):
                apart(s_gt, b * 2 + 2)
                load_x(xs, b + 1, s_x)
                apart(s_out, (b + 1) * NG * 16)
                apart(s_st, (b + 1) * NQ * STEPS + STEPS)
                load_x(y, b + 1, s_xr)

            pool.wait_ge(s_init, SETUP_DVE)
            residual(0)
            pool.wait_ge(s_at, 2)
            for n in range(NOW, len(PIECES)):
                load_piece(n, late, s_late)
                pool.wait_ge(s_late, 16 * (n - NOW + 1))
                split_piece(n, late)
            shared_bias(0)
            next_x(0)
            with pool.Fori(1, B - 1) as b:
                residual(b)
                shared_bias(b)
                next_x(b)
            residual(B - 1)
            shared_bias(B - 1)

        @block.scalar
        def _(act):
            def high_parts(dst, src_ready, base, done, scale, banks=(0, 1, 2, 3)):
                for n in range(4):
                    k, half = n % 2, n // 2
                    act.wait_ge(src_ready, base + n + 1)
                    act.activation(dst[:, k, 512 * half:512 * half + 512], ps[:, banks[n], :], ACT.Copy,
                                   scale=scale)\
                       .then_inc(done, 1)

            for j in range(2):
                act.dma_start(browraw[NC + 2 * j:NC + 2 * j + 2, :].rearrange("c (t f) -> c t f", t=4), b_qk[j])\
                   .then_inc(s_first, 16)
            act.dma_start(wraw[:, 6:8, :], w_out.rearrange("(c p) d -> p c d", p=128)).then_inc(s_first, 16)
            act.dma_start(browraw[NC + 4:NC + 6, :], b_qkv[2 * D:3 * D].rearrange("(k p) -> k p", p=128))\
               .then_inc(s_first, 16)
            act.dma_start(bo[:, :], b_out.partition_broadcast(128)).then_inc(s_small, 16)
            high_parts(wth, s_wt, 0, s_wth, SW)
            act.wait_ge(s_wt, 5)
            for k in range(3):
                cols = slice((0, NC, NC + 4)[k], (NC, NC + 4, NC + 6)[k])
                act.activation(bcol[:, cols], ps[:, 4, cols], ACT.Copy, scale=(1.0, SQ, SX)[k]).then_inc(s_bias, 1)
            act.wait_ge(s_bias, 3)

            def x_high(b):
                high_parts(tokh, s_xt, b * 4, s_xh, SX, XBANK)

            def normalized(dst, first, last, done):
                for t in range(first, last):
                    act.activation(dst[:, t, :], dst[:, t, :], ACT.Identity, bias=nmr[:, t:t + 1],
                                   scale=rstd[:, t:t + 1]).then_inc(done, 1)

            def second_std(b, half):
                act.wait_ge(s_var2, b * 2 + half + 1)
                act.activation(std[:, GB * half:GB * half + GB], mv[:, GB * half:GB * half + GB, 1], ACT.Sqrt)\
                   .then_inc(s_std2, 1)

            def second_norm(b, half):
                act.wait_ge(s_nm2, b * 2 + half + 1)
                normalized(y, (GB + GB // 2) * half, GB + GB * half, s_n2)

            def front(b, before=None):
                for n in range(8):
                    j = (2, 2, 3, 3, 0, 0, 1, 1)[n]
                    dst = (kh if n < 4 else qh)[:, j % 2, 512 * (n % 2):512 * (n % 2) + 512]
                    bias = bcol[:, NC + j:NC + j + 1]
                    act.wait_ge(s_prj, b * 12 + n + 1)
                    if n in HIGH_BY_ACT:
                        act.activation(dst, ps[:, 4 + n % 4, :], ACT.Identity, bias=bias,
                                       scale=SQ / (SX * SW)).then_inc(s_qkh, 1)
                    if n >= 2:
                        act.wait_ge(s_qkl, b * 8 + n - 1)
                    act.activation(proj[n % 2], ps[:, 4 + n % 4, :], ACT.Identity, bias=bias,
                                   scale=SQ / (SX * SW)).then_inc(s_q32, 1)
                    if before is not None and n == STD_AT:
                        second_std(before, 0)
                        second_std(before, 1)

            def rest(b, more):
                for n in range(4):
                    act.wait_ge(s_prj, b * 12 + 8 + n + 1)
                    act.activation(vs[:, 2 * n:2 * n + 2, :, 0:HD].rearrange("p t h d -> p (t h) d"),
                                   ps[:, 4 + n, :].rearrange("p (a d) -> p a d", d=HD), ACT.Copy,
                                   scale=1.0 / (SX * SW)).then_inc(s_v, 1)
                for it in range(NQ + 1):
                    def rows():
                        act.wait_ge(s_ring, b * RING + ring_after_rows(it))
                        if it >= 1:
                            p = it - 1
                            act.wait_ge(s_row[SLOT[p]], (b * PERB[SLOT[p]] + BEFORE[p] + 1) * 16 * ROW_DMAS)
                        act.activation(mrh[:, :], ps[0:32, (ring_after_rows(it) - 1) % 2, 0:TB], ACT.Copy,
                                       scale=-1.0 / SROW).then_inc(s_mrh, 1)

                    if it == 0:
                        rows()
                    if it >= 1:
                        for s in range(STEPS):
                            if it < NQ and s == ROWS_AT - LEAD:
                                rows()
                            n = (it - 1) * STEPS + s
                            u, hp = s // 2, s % 2
                            unit = (it - 1) * NU + u
                            w = 512 if UNITS[u] is None else 256 * len(UNITS[u])
                            act.wait_ge(s_st, b * NQ * STEPS + n + 1)
                            if unit >= 2:
                                act.wait_ge(s_pv, b * NQ * NU + unit - 1)
                            act.activation(pt[unit % 2][:, 2 * hp:2 * hp + 2, 0:w],
                                           ps[:, 2 + 2 * (n % 2):4 + 2 * (n % 2), 0:w], ACT.Exp,
                                           scale=HD**-0.5 / SQ**2).then_inc(s_exp, 1)
                        act.wait_ge(s_pv, b * NQ * NU + it * NU)
                        for half in range(2):
                            act.activation(oacc[:, 512 * half:512 * half + 512], ps[:, OUT0 + half, :], ACT.Copy)\
                               .then_inc(s_oacc, 1)
                for half in range(2):
                    act.wait_ge(s_at, b * 2 + half + 1)
                    act.activation(ath[:, 1, 512 * half:512 * half + 512], ps[:, 2 + half, :], ACT.Copy, scale=SX)\
                       .then_inc(s_ah, 1)
                for half in range(2):
                    act.wait_ge(s_var, b * 2 + half + 1)
                    act.activation(std[:, 4 * half:4 * half + 4], mv[:, 4 * half:4 * half + 4, 1], ACT.Sqrt)\
                       .then_inc(s_std, 1)
                    if half == 0:
                        act.wait_ge(s_nm, b * 2 + 1)
                        normalized(y, 0, 4, s_y)
                high_parts(tokh, s_yt, b * 4, s_yh, SX)

                def gate_parts():
                    for n in range(2):
                        act.wait_ge(s_gt, b * 2 + n + 1)
                        act.activation(cwt[:, 512 * n:512 * n + 512], ps[:, 4 + n, :], ACT.Copy, scale=SC)\
                           .then_inc(s_cwh, 1)

                def silu(g, c, j):
                    fi = b * NG + g
                    act.wait_ge(s_u, fi * NC + c + 1)
                    if isinstance(c, int) and 2 <= c < NS + 2:
                        act.wait_ge(s_hl, fi * NC + c - 1)
                    elif not isinstance(c, int) or c >= NS + 2:
                        act.wait_ge(s_hc, fi * NR + c - NS - 1)
                    elif g > 0:
                        act.wait_ge(s_hc, fi * NR + c - 1)
                    bias = bcol[:, c:c + 1] if isinstance(c, int) else bcol[:, bass.ds(c, 1)]
                    act.activation(hs_[j % 2], ps[:, j % 2, :], ACT.Silu, bias=bias,
                                   scale=1.0 / (SX * SW)).then_inc(s_silu, 1)

                def high(g, c, j):
                    fi = b * NG + g
                    routed = not isinstance(c, int) or c >= NS
                    if routed:
                        act.wait_ge(s_hc, fi * NR + c - NS + 1)
                    if not isinstance(c, int) or c >= 4 or g > 0:
                        act.wait_ge(s_dn, fi * NC + c - 3)
                    if routed:
                        act.activation(hh[j % 4], hc[j % 4], ACT.Copy).then_inc(s_hh, 1)
                    else:
                        act.wait_ge(s_silu, fi * NC + c + 1)
                        act.activation(hh[j % 4], hs_[j % 2], ACT.Copy, scale=SC).then_inc(s_hh, 1)

                for c in range(2):
                    silu(0, c, c)
                    high(0, c, c)
                act.wait_ge(s_rt, b * NR_ROUTER + 3)
                act.activation(lg[:, :, :], lg[:, :, :], ACT.Exp).then_inc(s_e, 1)
                for g in range(NG):
                    for c in range(NS + 4):
                        if g == 0 and c == GATES_AT + 1:
                            gate_parts()
                        if g > 0 or c >= 1:
                            silu(g, c + 1, c + 1)
                        if g > 0 or c >= 2:
                            high(g, c, c)
                    with act.Fori(NS // 4 + 1, NC // 4 - 1) as it:
                        for j in range(4):
                            silu(g, it * 4 + j + 1, j + 1)
                            high(g, it * 4 + j, j)
                    for c in range(NC - 4, NC):
                        if c + 1 < NC:
                            silu(g, c + 1, c + 1)
                        elif g + 1 < NG:
                            silu(g + 1, 0, 0)
                        high(g, c, c)
                if more:
                    x_high(b + 1)

            x_high(0)
            act.wait_ge(s_init, 2 * NSLOT + 1)
            for k in range(KD):
                act.activation(reph[:, k, :], zero[:, :], ACT.Identity, bias=bcol[:, NC + 4 + k:NC + 5 + k])\
                   .then_inc(s_rep, 1)
            front(0)
            with act.Fori(0, B - 1) as b:
                rest(b, True)
                front(b + 1, b)
                second_norm(b, 0)
                second_norm(b, 1)
            rest(B - 1, False)
            second_std(B - 1, 0)
            second_norm(B - 1, 0)
            second_std(B - 1, 1)
            second_norm(B - 1, 1)

        @block.vector
        def _(dve):
            steps = [0]

            def init(ins):
                steps[0] += 1
                ins.then_inc(s_init, 1)

            def apart(signal, value):
                if not isinstance(value, int):
                    value = dve.to_reg(value)
                    dve.wait_ge(s_init, SETUP_DVE)
                dve.wait_ge(signal, value)

            def low_parts(dst, high, high_done, base, done, scale, banks=(0, 1, 2, 3)):
                for n in range(4):
                    k, half = n % 2, n // 2
                    cols = slice(512 * half, 512 * half + 512)
                    dve.wait_ge(high_done, base + n + 1)
                    dve.scalar_tensor_tensor(dst[:, k, cols], ps[:, banks[n], :], scale, high[:, k, cols],
                                             ALU.mult, ALU.subtract).then_inc(done, 1)

            init(dve.memset(zero[:, :], 0.0))
            init(dve.memset(srow[:, :], SROW))
            for s in range(NSLOT):
                init(dve.memset(qs[s][:, :, :].rearrange("p a n -> p (a n)").bitcast(u32), 0))
                if s < NSLOT - 1:
                    init(dve.memset(ks[s][:, :, :].rearrange("p a n -> p (a n)").bitcast(u32), 0))
            assert steps[0] == 2 * NSLOT + 1
            low_parts(wtl, wth, s_wth, 0, s_wtl, SW)
            dve.memset(ps[:, OUT0:OUT0 + 2, :], 0.0).then_inc(s_ofree, 1)

            def x_low(b):
                low_parts(tokl, tokh, s_xh, b * 4, s_xl, SX, XBANK)

            def front(b, before=None):
                for n in range(8):
                    c, half = (n // 2) % 2, n % 2
                    high, low = (kh, kl) if n < 4 else (qh, ql)
                    cols = slice(512 * half, 512 * half + 512)
                    dve.wait_ge(s_q32, b * 8 + n + 1)
                    if n not in HIGH_BY_ACT:
                        own = sum(p not in HIGH_BY_ACT for p in range(n + 1))
                        dve.tensor_copy(high[:, c, cols], proj[n % 2]).then_inc(s_qkd, 1)
                        dve.wait_ge(s_qkd, b * (8 - len(HIGH_BY_ACT)) + own)
                    dve.tensor_tensor(low[:, c, cols], proj[n % 2], high[:, c, cols], ALU.subtract)\
                       .then_inc(s_qkl, 1)
                    if before is not None and n == min(STD_AT + 1, 7):
                        norm_scale(0, GB, before * 2, s_std2, s_rstd2, s_nm2)
                        second_norm(before)

            def norm_stats(first, last, b, ready, stats, aggregated):
                for t in range(first, last):
                    ready(t)
                    dve.bn_stats(bst[:, t, :], y[:, t, :]).then_inc(stats, 1)
                for t in range(first, last):
                    apart(stats, b * NB + t + 1)
                    dve.bn_aggr(mv[:, t, :], bst[:, t, :]).then_inc(aggregated, 1)

            def norm_variance(first, last, aggregated, count, var):
                dve.wait_ge(aggregated, count)
                dve.tensor_scalar(mv[:, first:last, 1], mv[:, first:last, 1], EPS, None, ALU.add).then_inc(var, 1)

            def norm_scale(first, last, b, std_ready, recip, shift):
                dve.wait_ge(std_ready, b + 1)
                dve.reciprocal(rstd[:, first:last], std[:, first:last]).then_inc(recip, 1)
                dve.wait_ge(recip, b + 1)
                dve.scalar_tensor_tensor(nmr[:, first:last], mv[:, first:last, 0], -1.0, rstd[:, first:last],
                                         ALU.mult, ALU.mult).then_inc(shift, 1)

            def second_stats(b, g):
                def ready(t):
                    if t % GB < GB - 1:
                        apart(s_z2, (b * NG + g) * (GB - 1) + t % GB + 1)
                    else:
                        apart(s_ofree, b * NG + g + 2)
                norm_stats(g * GB, g * GB + GB, b, ready, s_bs2, s_ba2)

            def second_norm(b):
                norm_scale(GB, NB, b * 2 + 1, s_std2, s_rstd2, s_nm2)
                for t in range(GB, GB + GB // 2):
                    dve.wait_ge(s_nm2, b * 2 + 2)
                    dve.tensor_scalar(y[:, t, :], y[:, t, :], rstd[:, t:t + 1], nmr[:, t:t + 1],
                                      ALU.mult, ALU.add).then_inc(s_n2v, 1)

            x_low(0)
            dve.wait_ge(s_rep, KD)
            for k in range(KD):
                dve.scalar_tensor_tensor(repl[:, k, :], zero[:, :], bcol[:, NC + 4 + k:NC + 5 + k], reph[:, k, :],
                                         ALU.add, ALU.subtract).then_inc(s_rep, 1)
            front(0)
            dve.wait_ge(s_small, SMALL)
            init(dve.memset(vs[:, :, :, :].rearrange("p t h d -> p (t h) d")[:, :, HD:HD + 1], 1.0))
            init(dve.tensor_tensor(sb2s[:, :], sb2s[:, :], sbraw, ALU.add))
            init(dve.tensor_scalar(rwh[:, :, :], rraw, SW, None, ALU.mult))
            init(dve.tensor_scalar(b2h[:, :], b2raw, SW, None, ALU.mult))
            dve.wait_ge(s_init, steps[0])
            init(dve.scalar_tensor_tensor(rwl[:, :, :], rraw, SW, rwh[:, :, :], ALU.mult, ALU.subtract))
            init(dve.scalar_tensor_tensor(b2l[:, :], b2raw, SW, b2h[:, :], ALU.mult, ALU.subtract))
            assert steps[0] == SETUP_DVE
            dve.wait_ge(s_bvo, 1)
            dve.scalar_tensor_tensor(bo[:, :], ps[:, 2, 0:D], 1.0 / (SX * SW), bo[:, :], ALU.mult, ALU.add)\
               .then_inc(s_bo, 1)

            def rest(b, more):
                ring = 0

                def normalize(q, half):
                    o = ps[:, ring % 2, :].rearrange("p (t g d) -> p t g d", t=4, g=4)
                    n = 2 * q + half
                    dve.wait_ge(s_ring, b * RING + ring + 1)
                    dve.reciprocal(rc[:, half, :, :], o[:, :, :, HD]).then_inc(s_rc, 1)
                    dve.wait_ge(s_rc, b * 2 * NQ + n + 1)
                    dve.tensor_tensor(
                        att[:, 4 * half:4 * half + 4, 64 * q:64 * q + 64].rearrange("p t (g d) -> p t g d", g=4),
                        o[:, :, :, 0:HD], rc[:, half, :, :].unsqueeze(3).to_broadcast([128, 4, 4, HD]),
                        ALU.mult).then_inc(s_free, 1)

                for it in range(NQ + 1):
                    for s in range(STEPS):
                        if it < NQ:
                            for m in maxima_of(s):
                                pos, u = head_of(m), m % NU
                                dve.wait_ge(s_ring, b * RING + ring + 1)
                                if UNITS[u] is None:
                                    dst, src = mxp[:, pos, u:u + 1], ps[:, ring_bank(ring), :]
                                else:
                                    k = len(UNITS[u])
                                    dst = mx[:, pos, UNITS[u][0]:UNITS[u][0] + k]
                                    src = ps[:, ring_bank(ring), 0:256 * k].rearrange("p (a n) -> p a n", n=256)
                                dve.reduce_max(dst, src, axis=AX.X).then_inc(s_free, 1)
                                ring += 1
                        if s == BACK_AT and it >= 2:
                            for half in range(2):
                                normalize(it - 2, half)
                                ring += 1
                        if s == 3 and it == NQ:
                            for half in range(2):
                                cols = slice(512 * half, 512 * half + 512)
                                dve.wait_ge(s_ring, b * RING + ring + 1)
                                dve.tensor_scalar(ath[:, 0, cols], ps[:, ring % 2, :], SX, None, ALU.mult)\
                                   .then_inc(s_a0, 1)
                                dve.wait_ge(s_a0, b * 2 + half + 1)
                                dve.scalar_tensor_tensor(atl[:, 0, cols], ps[:, ring % 2, :], SX, ath[:, 0, cols],
                                                         ALU.mult, ALU.subtract).then_inc(s_free, 1)
                                ring += 1
                    if it < NQ:
                        dve.wait_ge(s_free, b * RING + ring)
                        dve.tensor_reduce(mx[:, :, 0:1].rearrange("p g o -> p (g o)"), mxp[:, :, :],
                                          axis=AX.X, op=ALU.max).then_inc(s_mx, 1)
                        dve.wait_ge(s_mrh, b * NQ + it + 1)
                        dve.scalar_tensor_tensor(mrl[:, :], ps[0:32, ring % 2, 0:TB], -1.0 / SROW, mrh[:, :],
                                                 ALU.mult, ALU.subtract).then_inc(s_free, 1)
                        ring += 1
                        assert ring == ring_after_rows(it)
                for half in range(2):
                    normalize(NQ - 1, half)
                    ring += 1
                assert ring == RING

                for half in range(2):
                    cols = slice(512 * half, 512 * half + 512)
                    dve.wait_ge(s_ah, b * 2 + half + 1)
                    dve.scalar_tensor_tensor(atl[:, 1, cols], ps[:, 2 + half, :], SX, ath[:, 1, cols],
                                             ALU.mult, ALU.subtract).then_inc(s_al, 1)
                dve.wait_ge(s_xb, b + 1)
                for half in range(2):
                    for t in range(4 * half, 4 * half + 4):
                        dve.wait_ge(s_op, b * 4 + t // 2 + 1)
                        dve.scalar_tensor_tensor(y[:, t, :], ps[:, 4 + t // 2, 256 * (t % 2):256 * (t % 2) + 256],
                                                 1.0 / (SX * SW), y[:, t, :], ALU.mult, ALU.add)\
                           .then_inc(s_z, 1)
                        if t == SCALE_AT:
                            norm_scale(0, 4, b * 2, s_std, s_rstd, s_nm)
                    norm_stats(4 * half, 4 * half + 4, b, lambda t: dve.wait_ge(s_z, b * NB + t + 1),
                               s_bs, s_ba)
                    norm_variance(4 * half, 4 * half + 4, s_ba, b * NB + 4 * half + 4, s_var)
                norm_scale(4, NB, b * 2 + 1, s_std, s_rstd, s_nm)
                dve.wait_ge(s_nm, b * 2 + 2)
                for t in range(4, NB):
                    dve.tensor_scalar(y[:, t, :], y[:, t, :], rstd[:, t:t + 1], nmr[:, t:t + 1],
                                      ALU.mult, ALU.add).then_inc(s_yv, 1)
                low_parts(tokl, tokh, s_yh, b * 4, s_yl, SX)

                def gated(g, c, j):
                    fi = b * NG + g
                    dve.wait_ge(s_silu, fi * NC + c + 1)
                    dve.wait_ge(s_cwb, fi * NR + c - NS + 1)
                    dve.tensor_tensor(hc[j % 4], hs_[j % 2], ps[:, 2 + j % 2, :], ALU.mult).then_inc(s_hc, 1)

                def low(g, c, j):
                    dve.wait_ge(s_hh, (b * NG + g) * NC + c + 1)
                    if not isinstance(c, int) or c >= NS:
                        dve.tensor_tensor(hl[j % 4], hc[j % 4], hh[j % 4], ALU.subtract).then_inc(s_hl, 1)
                    else:
                        dve.scalar_tensor_tensor(hl[j % 4], hs_[j % 2], SC, hh[j % 4],
                                                 ALU.mult, ALU.subtract).then_inc(s_hl, 1)

                dve.wait_ge(s_lg, b + 1)
                dve.scalar_tensor_tensor(lg[:, :, :], ps[:, 4, :].rearrange("p (t e) -> p t e", e=E),
                                         1.0 / (SX * SW), rb[:, :].unsqueeze(1).to_broadcast([128, NB, E]),
                                         ALU.mult, ALU.add).then_inc(s_rt, 1)
                dve.wait_ge(s_rt, b * NR_ROUTER + 1)
                dve.reduce_max(rmax[:, :], lg[:, :, :], axis=AX.X).then_inc(s_rt, 1)
                dve.wait_ge(s_rt, b * NR_ROUTER + 2)
                dve.tensor_tensor(lg[:, :, :], lg[:, :, :], rmax[:, :].unsqueeze(2).to_broadcast([128, NB, E]),
                                  ALU.subtract).then_inc(s_rt, 1)
                low(0, 0, 0)
                low(0, 1, 1)
                apart(s_e, b + 1)
                for t in range(NB):
                    dve.max(top[:, t, :], lg[:, t, :]).then_inc(s_top, 1)
                apart(s_top, b * 2 * NB + NB)
                for t in range(NB):
                    dve.match_replace(untop[:, t, :], top[:, t, :], lg[:, t, :], -1.0).then_inc(s_top, 1)
                dve.tensor_reduce(nsum[:, :], top[:, :, :], axis=AX.X, op=ALU.add, negate=True)\
                   .then_inc(s_rt, 1)
                low(0, 2, 2)
                dve.wait_ge(s_top, b * 2 * NB + 2 * NB)
                dve.wait_ge(s_rt, b * NR_ROUTER + 4)
                dve.reciprocal(nsum[:, :], nsum[:, :]).then_inc(s_rt, 1)
                dve.scalar_tensor_tensor(untop[:, :, :], untop[:, :, :], 0.0, lg[:, :, :],
                                         ALU.max, ALU.subtract).then_inc(s_rt, 1)
                dve.wait_ge(s_rt, b * NR_ROUTER + 6)
                for n in range(2):
                    dve.tensor_tensor(gate[:, :, E * n:E * n + E], untop[:, :, :],
                                      nsum[:, :].unsqueeze(2).to_broadcast([128, NB, E]), ALU.mult)\
                       .then_inc(s_gate, 1)
                low(0, 3, 3)
                low(0, 4, 4)
                for n in range(2):
                    cols = slice(512 * n, 512 * n + 512)
                    dve.wait_ge(s_cwh, b * 2 + n + 1)
                    dve.scalar_tensor_tensor(cwt[E:2 * E, cols], ps[E:2 * E, 4 + n, :], SC, cwt[E:2 * E, cols],
                                             ALU.mult, ALU.subtract).then_inc(s_cwl, 1)

                for g in range(NG):
                    for c in range(NS):
                        if c == NS - 1:
                            gated(g, NS, NS)
                        if g > 0 or c > GATES_AT:
                            low(g, c, c)
                        if g > 0 and c == NS // 2:
                            second_stats(b, g - 1)
                            norm_variance(0, GB, s_ba2, b * NB + GB, s_var2)
                    with dve.Fori(NS // 4, NC // 4 - 1) as it:
                        for j in range(4):
                            gated(g, it * 4 + j + 1, j + 1)
                            low(g, it * 4 + j, j)
                    for c in range(NC - 4, NC):
                        if c + 1 < NC:
                            gated(g, c + 1, c + 1)
                        low(g, c, c)
                    if g == NG - 1:
                        if more:
                            x_low(b + 1)
                        else:
                            norm_scale(0, GB, b * 2, s_std2, s_rstd2, s_nm2)
                    if g == 0:
                        dve.wait_ge(s_yb, b + 1)
                    dve.wait_ge(s_dn, (b * NG + g + 1) * NC)
                    for t in range(GB):
                        z = dve.scalar_tensor_tensor(
                            y[:, g * GB + t, :], ps[:, OUT0 + t // 2, 256 * (t % 2):256 * (t % 2) + 256],
                            1.0 / (SC * SW), y[:, g * GB + t, :], ALU.mult, ALU.add)
                        z.then_inc(s_z2 if t < GB - 1 else s_ofree, 1)
                second_stats(b, NG - 1)
                norm_variance(GB, NB, s_ba2, b * NB + NB, s_var2)

            with dve.Fori(0, B - 1) as b:
                rest(b, True)
                front(b + 1, b)
            rest(B - 1, False)
            second_norm(B - 1)

        @block.tensor
        def _(pe):
            def transposed(src, done):
                for n in range(4):
                    k, half = n % 2, n // 2
                    for t in range(4):
                        last = pe.transpose(ps[:, n, 128 * t:128 * t + 128],
                                            src[:, 4 * half + t, 128 * k:128 * k + 128], ident[:, :])
                    last.then_inc(done, 1)

            def parts(dst, stationary, moving, start=True, stop=True, skip=False):
                terms = [(s, m) for k in range(len(stationary[0]))
                         for s, m in ((stationary[0][k], moving[0][k]), (stationary[0][k], moving[1][k]),
                                      (stationary[1][k], moving[0][k]))]
                for n, (s, m) in enumerate(terms):
                    last = pe.matmul(dst, s, m, start=start and n == 0, stop=stop and n == len(terms) - 1,
                                     skip_group_check=skip)
                return last

            pe.wait_ge(s_ident, 1)
            pe.wait_ge(s_first, FIRST)
            transposed(wraw, s_wt)
            pe.transpose(ps[:, 4, 0:NC + 6], browraw, ident[0:NC + 6, 0:NC + 6]).then_inc(s_wt, 1)
            pe.wait_ge(s_wtl, 4)

            def x_transposed(half):
                for k in range(KD):
                    for t in range(4):
                        last = pe.transpose(ps[:, XBANK[2 * half + k], 128 * t:128 * t + 128],
                                            xs[:, 4 * half + t, 128 * k:128 * k + 128], ident[:, :])
                    last.then_inc(s_xt, 1)

            def projections(b):
                for n in range(8):
                    if n < 2:
                        pe.wait_ge(s_xl, b * 4 + 2 * n + 2)
                    j = (2, 2, 3, 3, 0, 0, 1, 1)[n]
                    half = n % 2
                    if n == 2:
                        pe.wait_ge(s_ofree, b * NG + 1)
                    if n >= 4:
                        pe.wait_ge(s_q32, b * 8 + n - 3)
                    cols = slice(512 * half, 512 * half + 512)
                    parts(ps[:, 4 + n % 4, :],
                          [[w[:, k, 128 * j:128 * j + 128] for k in range(KD)] for w in (wth, wtl)],
                          [[m[:, k, cols] for k in range(KD)] for m in (tokh, tokl)]).then_inc(s_prj, 1)

            def rest(b, more):
                def value_block(t):
                    if t % 2 == 0:
                        pe.wait_ge(s_q32, b * 8 + 4 + t // 2 + 1)
                    toks = slice(TB * t, TB * t + TB)
                    last = parts(ps[:, 4 + t // 2, 256 * (t % 2):256 * (t % 2) + 256],
                                 [[m[:, k, toks] for k in range(KD)] for m in (tokh, tokl)],
                                 [[w[:, k, 512:768] for k in range(KD)] for w in (wth, wtl)])
                    if t % 2:
                        last.then_inc(s_prj, 1)

                ring = 0

                def maxima_unit(q, m):
                    pos, u = head_of(m), m % NU
                    pr = place(pos)[1]
                    slot = SLOT[q]
                    if ring >= MU:
                        pe.wait_ge(s_free, b * RING + ring - 1)
                    elif ring >= 4:
                        pe.wait_ge(s_free, b * RING + ring - 3)
                    bank = ring_bank(ring)
                    if UNITS[u] is None:
                        last = pe.matmul(ps[:, bank, :], qs[slot][:, pr, 0:TB],
                                         ks[slot][:, pos, 512 * u:512 * u + 512], start=True, stop=True)
                    else:
                        for n, i in enumerate(UNITS[u]):
                            last = pe.matmul(ps[:, bank, 256 * n:256 * n + 256],
                                             qs[slot][:, pr, TB * i:TB * i + TB],
                                             blocks(ks[slot][:, pos, :], i), start=True, stop=True)
                    last.then_inc(s_ring, 1)

                def rows(q):
                    pe.wait_ge(s_mx, b * NQ + q + 1)
                    pe.wait_ge(s_free, b * RING + ring - 1)
                    pe.transpose(ps[0:32, ring % 2, 0:TB], mx[:, :, :].rearrange("p g t -> p (g t)"),
                                 ident[:, :]).then_inc(s_ring, 1)

                def scores(q, s):
                    n = q * STEPS + s
                    u, hp = s // 2, s % 2
                    slot = SLOT[q]
                    if n >= 2:
                        pe.wait_ge(s_exp, b * NQ * STEPS + n - 1)
                    for a in range(2):
                        pos = 2 * hp + a
                        pr = place(pos)[1]
                        bank = 2 + 2 * (n % 2) + a
                        if UNITS[u] is None:
                            last = pe.matmul(ps[:, bank, :], ks[slot][:, pos, 0:TB],
                                             qs[slot][:, pr, 512 * u:512 * u + 512], start=True, stop=True)
                        else:
                            for m, i in enumerate(UNITS[u]):
                                last = pe.matmul(ps[:, bank, 256 * m:256 * m + 256],
                                                 ks[slot][:, pos, TB * i:TB * i + TB],
                                                 blocks(qs[slot][:, pr, :], i), start=True, stop=True)
                    last.then_inc(s_st, 1)

                def sum_values(q, u):
                    unit = q * NU + u
                    pe.wait_ge(s_exp, b * NQ * STEPS + q * STEPS + 2 * u + 2)
                    if u == 0 and q >= 1:
                        pe.wait_ge(s_oacc, (b * NQ + q) * 2)
                    end = u == NU - 1
                    products = []
                    if UNITS[u] is None:
                        products.append((0, OUT0 + u, slice(0, 512), slice(0, 512), True, False))
                    else:
                        for m, i in enumerate(UNITS[u]):
                            bank, col = OUT0 + i // 4, TB * (i % 4)
                            products.append((i, OUT0, slice(0, TB), slice(256 * m, 256 * m + TB), False, end))
                            products.append((i, bank, slice(col, col + TB),
                                             slice(256 * m + TB, 256 * m + 256), False, end))
                    for i, bank, dst, src, start, stop in products:
                        for g in range(4):
                            pos = 2 * (g % 2) + g // 2
                            last = pe.matmul(ps[32 * g:32 * g + HD + 1, bank, dst], vs[:, i, 4 * q + g, :],
                                             pt[unit % 2][:, pos, src], start=start, stop=stop,
                                             skip_group_check=True)
                    last.then_inc(s_pv, 1)

                def output_back(q):
                    nonlocal ring
                    for half in range(2):
                        pe.wait_ge(s_oacc, (b * NQ + q) * 2 + half + 1)
                        pe.wait_ge(s_free, b * RING + ring - 1)
                        for t in range(4):
                            cols = slice(TB * (4 * half + t), TB * (4 * half + t) + TB)
                            last = pe.transpose(ps[:, ring % 2, TB * t:TB * t + TB], oacc[:, cols], ident[:, :])
                        last.then_inc(s_ring, 1)
                        ring += 1

                for t in range(VALUES_FIRST):
                    value_block(t)
                pe.wait_ge(s_bo, 1)
                for it in range(NQ + 1):
                    for s in range(STEPS + LEAD):
                        if it < NQ and s < STEPS:
                            if s == (STEPS // 2 if it == 0 else 0):
                                pe.wait_ge(s_stk[SLOT[it]], stack_loads(b, it))
                            elif s == 0:
                                pe.wait_ge(s_half, (b + 1) * FIRST_HALF * 16)
                            units = maxima_of(s)
                            for m in units[:1]:
                                maxima_unit(it, m)
                                ring += 1
                        else:
                            units = ()
                        if 0 < it < NQ and s == ROWS_AT:
                            rows(it)
                            ring += 1
                        if it >= 1 and s >= LEAD:
                            q, r = it - 1, s - LEAD
                            if r == 0:
                                if q == 0:
                                    pe.wait_ge(s_v, b * 4 + 4)
                                pe.wait_ge(s_row[SLOT[q]],
                                           (b * PERB[SLOT[q]] + BEFORE[q] + 1) * 16 * ROW_DMAS)
                            scores(q, r)
                        for m in units[1:]:
                            maxima_unit(it, m)
                            ring += 1
                        if it == 0 and VALUES_FIRST + s < NB:
                            value_block(VALUES_FIRST + s)
                        if s == 0 and it >= 2:
                            sum_values(it - 2, NU - 1)
                        if s == BACK_AT and it >= 2:
                            output_back(it - 2)
                        if s == 3 and it == NQ:
                            for half in range(2):
                                pe.wait_ge(s_free, b * RING + ring - 1)
                                for t in range(4):
                                    last = pe.transpose(ps[:, ring % 2, TB * t:TB * t + TB],
                                                        att[:, 4 * half + t, 0:128], ident[:, :])
                                last.then_inc(s_ring, 1)
                                ring += 1
                        if it >= 1 and s >= LEAD + 3 and (s - LEAD) % 2:
                            sum_values(it - 1, (s - LEAD - 3) // 2)
                    if it == 0:
                        rows(it)
                        ring += 1
                sum_values(NQ - 1, NU - 1)
                output_back(NQ - 1)
                assert ring == RING

                for half in range(2):
                    pe.wait_ge(s_free, b * RING + RING - 1 + half)
                    for t in range(4):
                        last = pe.transpose(ps[:, 2 + half, TB * t:TB * t + TB], att[:, 4 * half + t, 128:256],
                                            ident[:, :])
                    last.then_inc(s_at, 1)
                for t in range(NB):
                    pe.wait_ge(s_al, b * 2 + t // 4 + 1)
                    toks = slice(TB * t, TB * t + TB)
                    last = parts(ps[:, 4 + t // 2, 256 * (t % 2):256 * (t % 2) + 256],
                                 [[m[:, k, toks] for k in range(KD)] for m in (ath, atl)],
                                 [[w[:, k, 768:1024] for k in range(KD)] for w in (wth, wtl)])
                    if t % 2:
                        last.then_inc(s_op, 1)

                for n in range(4):
                    k, half = n % 2, n // 2
                    for t in range(4 * half, 4 * half + 4):
                        if half == 0:
                            pe.wait_ge(s_y, b * 4 + t + 1)
                        else:
                            pe.wait_ge(s_yv, b * 4 + t - 3)
                        last = pe.transpose(ps[:, n, 128 * (t % 4):128 * (t % 4) + 128],
                                            y[:, t, 128 * k:128 * k + 128], ident[:, :])
                    last.then_inc(s_yt, 1)
                pe.wait_ge(s_init, SETUP_DVE)
                for t in range(NB):
                    toks = slice(TB * t, TB * t + TB)
                    pe.wait_ge(s_yl, b * 4 + 2 * (t // 4) + 2)
                    last = parts(ps[:, 4, E * t:E * t + E],
                                 [[m[:, k, toks] for k in range(KD)] for m in (tokh, tokl)],
                                 [[w[:, k, :] for k in range(KD)] for w in (rwh, rwl)])
                last.then_inc(s_lg, 1)

                def up(g, c, j):
                    cols = slice(128 * c, 128 * c + 128) if isinstance(c, int) else bass.ds(c * 128, 128)
                    toks = slice(GT * g, GT * g + GT)
                    if not isinstance(c, int) or c >= 2 or g > 0:
                        pe.wait_ge(s_silu, (b * NG + g) * NC + c - 1)
                    parts(ps[:, j % 2, :], [[w[:, k, cols] for k in range(KD)] for w in (w1h, w1l)],
                          [[m[:, k, toks] for k in range(KD)] for m in (tokh, tokl)]).then_inc(s_u, 1)

                def spread(g, c, j):
                    if not isinstance(c, int) or c >= NS + 2 or g > 0:
                        pe.wait_ge(s_hc, (b * NG + g) * NR + c - NS - 1)
                    one = sel[:, c - NS, :] if isinstance(c, int) else \
                        sel[:, bass.ds(c - NS, 1), :].rearrange("p o m -> p (o m)")
                    pe.matmul(ps[:, 2 + j % 2, :], one, cwt[:, GT * g:GT * g + GT],
                              start=True, stop=True).then_inc(s_cwb, 1)

                def gated_bias(g):
                    for t in range(GB):
                        toks = cwt[:, GT * g + TB * t:GT * g + TB * t + TB]
                        dst = ps[:, OUT0 + t // 2, 256 * (t % 2):256 * (t % 2) + 256]
                        for part in (b2h, b2l):
                            pe.matmul(dst, toks, part[:, :], start=False, stop=False, skip_group_check=True)

                def down(g, c, j, end=False):
                    first = isinstance(c, int) and c == 0
                    if first:
                        pe.wait_ge(s_ofree, b * NG + g + 1)
                    pe.wait_ge(s_hl, (b * NG + g) * NC + c + 1)
                    for t in range(GB):
                        toks = slice(TB * t, TB * t + TB)
                        if isinstance(c, int):
                            ws = [w[:, c, :] for w in (w2h, w2l)]
                        else:
                            ws = [w[:, bass.ds(c, 1), :].rearrange("p o d -> p (o d)") for w in (w2h, w2l)]
                        last = parts(ps[:, OUT0 + t // 2, 256 * (t % 2):256 * (t % 2) + 256],
                                     [[h[j % 4][:, toks]] for h in (hh, hl)], [[w] for w in ws],
                                     start=first and t % 2 == 0, stop=end, skip=True)
                    last.then_inc(s_dn, 1)

                pe.wait_ge(s_wstep, 3 * NOW)
                pe.wait_ge(s_setup, 4)
                up(0, 0, 0)
                up(0, 1, 1)
                for g in range(NG):
                    for c in range(NS):
                        if g == 0 and c == GATES_AT:
                            pe.wait_ge(s_gate, b * 2 + 2)
                            for n in range(2):
                                for t in range(4):
                                    last = pe.transpose(ps[:, 4 + n, TB * t:TB * t + TB], gate[:, 4 * n + t, :],
                                                        ident[:, :])
                                last.then_inc(s_gt, 1)
                        up(g, c + 2, c)
                        if c + 2 >= NS:
                            if g == 0 and c + 2 == NS:
                                pe.wait_ge(s_cwl, b * 2 + 2)
                            spread(g, c + 2, c)
                        down(g, c, c)
                    gated_bias(g)
                    if g == 0:
                        pe.wait_ge(s_wstep, 3 * len(PIECES))
                    with pe.Fori(NS // 4, NC // 4 - 1) as it:
                        for j in range(4):
                            up(g, it * 4 + j + 2, j)
                            spread(g, it * 4 + j + 2, j)
                            down(g, it * 4 + j, j)
                    for c in range(NC - 4, NC):
                        if c + 2 < NC:
                            up(g, c + 2, c)
                            spread(g, c + 2, c)
                        elif g + 1 < NG:
                            up(g + 1, c + 2 - NC, c)
                        elif c == NC - 2 and more:
                            pe.wait_ge(s_x, b * 16 + 32)
                            x_transposed(0)
                        elif c == NC - 1 and more:
                            pe.wait_ge(s_silu, (b * NG + NG) * NC)
                            x_transposed(1)
                        down(g, c, c, c == NC - 1)

            pe.wait_ge(s_x, 16)
            pe.wait_ge(s_bias, 3)
            x_transposed(0)
            x_transposed(1)
            projections(0)
            pe.wait_ge(s_rep, 2 * KD)
            parts(ps[:, 2, 0:D], [[m[:, k, :] for k in range(KD)] for m in (reph, repl)],
                  [[w[:, k, 768:1024] for k in range(KD)] for w in (wth, wtl)]).then_inc(s_bvo, 1)
            with pe.Fori(0, B - 1) as b:
                rest(b, True)
                projections(b + 1)
            rest(B - 1, False)


_INS = ['L0_attn_x', 'L0_attn_w_qkv', 'L0_attn_b_qkv', 'L0_attn_w_out', 'L0_attn_b_out',
        'L0_ffn_router_w', 'L0_ffn_router_b', 'L0_ffn_w1', 'L0_ffn_b1', 'L0_ffn_w2', 'L0_ffn_b2',
        'L0_ffn_sw1', 'L0_ffn_sb1', 'L0_ffn_sw2', 'L0_ffn_sb2']
_OUTS = [((4, 1024, 256), 'float32')]


def kernel(**inputs):
    import numpy as _np
    import concourse.bacc as _bacc
    from concourse import mybir as _mybir
    from concourse.bass_utils import run_bass_kernel_spmd as _run

    nc = _bacc.Bacc("TRN2", target_bir_lowering=False, num_devices=1)
    arrays, args = {}, []
    for name in _INS:
        a = _np.ascontiguousarray(inputs[name])
        arrays[f"in_{name}_dram"] = a
        args.append(nc.dram_tensor(f"in_{name}_dram", a.shape, _mybir.dt.from_np(a.dtype), kind="ExternalInput").ap())
    for i, (shape, dtype) in enumerate(_OUTS):
        dt = _mybir.dt.from_np(_np.dtype(dtype))
        args.append(nc.dram_tensor(f"out_{i}_dram", shape, dt, kind="ExternalOutput").ap())
    post_ln_block_kernel(nc, *args)
    r = _run(nc, [arrays], core_ids=[0])
    return r.results[0]["out_0_dram"]
```
